# Optimizing a Trainium2 kernel written in Bass

```python
import numpy as np
import jax
import jax.numpy as jnp

def _softmax(x, axis=-1):
    return jax.nn.softmax(x, axis=axis)

def _gelu(x):
    return jax.nn.gelu(x, approximate=True)

def _silu(x):
    return jax.nn.silu(x)

def _sigmoid(x):
    return jax.nn.sigmoid(x)

def _layernorm(x, axis=-1, eps=1e-05):
    m = jnp.mean(x, axis=axis, keepdims=True)
    v = jnp.var(x, axis=axis, keepdims=True)
    return (x - m) / jnp.sqrt(v + eps)

def _scatter_add(tgt, idx, src, axis=0):
    return tgt.at[idx].add(src)

def _segment_sum(src, seg, n):
    return jax.ops.segment_sum(src, seg, n)
kernel_name = 'mk_adaln_d1_jaxref_r4_d5e255'

def setup_inputs(seed: int=0):
    np.random.seed(seed)
    _w = jnp.asarray

    def _L0_attn_setup():
        import jax, jax.numpy as jnp
        import numpy as np
        HIDDEN = 256
        EXPAND = 1
        INPUT_DIM = HIDDEN * EXPAND
        CONV_K = 4
        NORM_EPS = 1e-05

        def causal_depthwise_conv(x, w):
            B, T, D = x.shape
            K = w.shape[1]
            xp = jnp.pad(x, ((0, 0), (K - 1, 0), (0, 0)))
            out = jnp.zeros_like(x)
            for k in range(K):
                out = out + xp[:, k:k + T, :] * w[:, k]
            return out

        def hgrn_forward(x, Wi, Wf, Wg, conv_i, conv_f, g_norm_weight, Wo):
            B, T, H = x.shape
            i_raw = jnp.einsum('bth,hd->btd', x, Wi)
            f_raw = jnp.einsum('bth,hd->btd', x, Wf)
            g_raw = jnp.einsum('bth,hd->btd', x, Wg)
            i_raw = causal_depthwise_conv(i_raw, conv_i)
            f_raw = causal_depthwise_conv(f_raw, conv_f)
            forget_gate = jax.nn.sigmoid(f_raw)
            i = jax.nn.silu(i_raw) * (1.0 - forget_gate)

            def step(h, fi):
                f_t, i_t = fi
                h = f_t * h + i_t
                return (h, h)
            h0 = jnp.zeros((B, i.shape[-1]), dtype=x.dtype)
            _, o_rec = jax.lax.scan(step, h0, (forget_gate.swapaxes(0, 1), i.swapaxes(0, 1)))
            o_rec = o_rec.swapaxes(0, 1)
            rms = jax.lax.rsqrt(jnp.mean(o_rec * o_rec, axis=-1, keepdims=True) + NORM_EPS)
            o = o_rec * rms * g_norm_weight * jax.nn.silu(g_raw)
            return jnp.einsum('btd,dh->bth', o, Wo)
        key = jax.random.key(seed)
        ks = jax.random.split(key, 8)
        B, T, H, D = (4, 512, HIDDEN, INPUT_DIM)
        s = 1.0 / np.sqrt(H)
        return {'x': jax.random.normal(ks[0], (B, T, H), dtype=jnp.float32), 'Wi': jax.random.normal(ks[1], (H, D), dtype=jnp.float32) * s, 'Wf': jax.random.normal(ks[2], (H, D), dtype=jnp.float32) * s, 'Wg': jax.random.normal(ks[3], (H, D), dtype=jnp.float32) * s, 'conv_i': jax.random.normal(ks[4], (D, CONV_K), dtype=jnp.float32) * 0.5, 'conv_f': jax.random.normal(ks[5], (D, CONV_K), dtype=jnp.float32) * 0.5, 'g_norm_weight': jnp.ones((D,), dtype=jnp.float32), 'Wo': jax.random.normal(ks[6], (D, H), dtype=jnp.float32) / np.sqrt(D)}
    _L0_attn_in = _L0_attn_setup()

    def _L0_ffn_setup():
        import jax, jax.numpy as jnp
        import numpy as np
        E = 8
        K = 2
        C = 256
        F = 512
        EPS = 1e-05
        key = jax.random.key(seed)
        ks = jax.random.split(key, 6)
        x = jax.random.normal(ks[0], (2, 256, C), dtype=jnp.float32)
        ln_gamma = 1.0 + 0.02 * jax.random.normal(ks[1], (C,), dtype=jnp.float32)
        ln_beta = 0.02 * jax.random.normal(ks[2], (C,), dtype=jnp.float32)
        gate_w = jax.random.normal(ks[3], (E, C), dtype=jnp.float32) / np.sqrt(C)
        w1 = jax.random.normal(ks[4], (E, F, C), dtype=jnp.float32) / np.sqrt(C)
        w2 = jax.random.normal(ks[5], (E, C, F), dtype=jnp.float32) / np.sqrt(F)
        return {'x': x, 'ln_gamma': ln_gamma, 'ln_beta': ln_beta, 'gate_w': gate_w, 'w1': w1, 'w2': w2}
    _L0_ffn_in = _L0_ffn_setup()
    _L0_c = _w((lambda *s: np.random.randn(*s).astype(np.float32) * 0.05)(16, 256))
    _L0_wmod = _w((lambda *s: np.random.randn(*s).astype(np.float32) * 0.05)(256, 6 * 256) * 256 ** (-0.5))
    _d = {'L0_attn_x': _L0_attn_in['x'], 'L0_attn_Wi': _L0_attn_in['Wi'], 'L0_attn_Wf': _L0_attn_in['Wf'], 'L0_attn_Wg': _L0_attn_in['Wg'], 'L0_attn_conv_i': _L0_attn_in['conv_i'], 'L0_attn_conv_f': _L0_attn_in['conv_f'], 'L0_attn_g_norm_weight': _L0_attn_in['g_norm_weight'], 'L0_attn_Wo': _L0_attn_in['Wo'], 'L0_ffn_ln_gamma': _L0_ffn_in['ln_gamma'], 'L0_ffn_ln_beta': _L0_ffn_in['ln_beta'], 'L0_ffn_gate_w': _L0_ffn_in['gate_w'], 'L0_ffn_w1': _L0_ffn_in['w1'], 'L0_ffn_w2': _L0_ffn_in['w2'], 'L0_c': _L0_c, 'L0_wmod': _L0_wmod}
    _x0 = _d['L0_attn_x']
    _d['L0_attn_x'] = jax.random.normal(jax.random.fold_in(jax.random.key(seed), 1), (16, 512, 256), dtype=_x0.dtype)
    del _x0
    return _d

def reference(L0_attn_x, L0_attn_Wi, L0_attn_Wf, L0_attn_Wg, L0_attn_conv_i, L0_attn_conv_f, L0_attn_g_norm_weight, L0_attn_Wo, L0_ffn_ln_gamma, L0_ffn_ln_beta, L0_ffn_gate_w, L0_ffn_w1, L0_ffn_w2, L0_c, L0_wmod):

    def _L0_attn_ref(x, Wi, Wf, Wg, conv_i, conv_f, g_norm_weight, Wo):
        import jax, jax.numpy as jnp
        import numpy as np
        HIDDEN = 256
        EXPAND = 1
        INPUT_DIM = HIDDEN * EXPAND
        CONV_K = 4
        NORM_EPS = 1e-05

        def causal_depthwise_conv(x, w):
            B, T, D = x.shape
            K = w.shape[1]
            xp = jnp.pad(x, ((0, 0), (K - 1, 0), (0, 0)))
            out = jnp.zeros_like(x)
            for k in range(K):
                out = out + xp[:, k:k + T, :] * w[:, k]
            return out

        def hgrn_forward(x, Wi, Wf, Wg, conv_i, conv_f, g_norm_weight, Wo):
            B, T, H = x.shape
            i_raw = jnp.einsum('bth,hd->btd', x, Wi)
            f_raw = jnp.einsum('bth,hd->btd', x, Wf)
            g_raw = jnp.einsum('bth,hd->btd', x, Wg)
            i_raw = causal_depthwise_conv(i_raw, conv_i)
            f_raw = causal_depthwise_conv(f_raw, conv_f)
            forget_gate = jax.nn.sigmoid(f_raw)
            i = jax.nn.silu(i_raw) * (1.0 - forget_gate)

            def step(h, fi):
                f_t, i_t = fi
                h = f_t * h + i_t
                return (h, h)
            h0 = jnp.zeros((B, i.shape[-1]), dtype=x.dtype)
            _, o_rec = jax.lax.scan(step, h0, (forget_gate.swapaxes(0, 1), i.swapaxes(0, 1)))
            o_rec = o_rec.swapaxes(0, 1)
            rms = jax.lax.rsqrt(jnp.mean(o_rec * o_rec, axis=-1, keepdims=True) + NORM_EPS)
            o = o_rec * rms * g_norm_weight * jax.nn.silu(g_raw)
            return jnp.einsum('btd,dh->bth', o, Wo)
        return hgrn_forward(x, Wi, Wf, Wg, conv_i, conv_f, g_norm_weight, Wo)

    def _L0_ffn_ref(x, ln_gamma, ln_beta, gate_w, w1, w2):
        import jax, jax.numpy as jnp
        import numpy as np
        E = 8
        K = 2
        C = 256
        F = 512
        EPS = 1e-05
        B, T, Cc = x.shape
        xf = x.reshape(-1, Cc)
        mu = jnp.mean(xf, axis=-1, keepdims=True)
        var = jnp.var(xf, axis=-1, keepdims=True)
        rn = (xf - mu) * jax.lax.rsqrt(var + EPS) * ln_gamma + ln_beta
        logits = rn @ gate_w.T
        probs = jax.nn.softmax(logits, axis=-1)
        rw, sel = jax.lax.top_k(probs, K)
        comb = jnp.sum(jax.nn.one_hot(sel, E, dtype=xf.dtype) * rw[..., None], axis=1)
        h = jax.nn.gelu(jnp.einsum('nc,efc->enf', xf, w1), approximate=False)
        y = jnp.einsum('enf,ecf->enc', h, w2)
        out = jnp.einsum('enc,ne->nc', y, comb)
        return out.reshape(B, T, Cc)
    x = L0_attn_x
    mod = (_silu(L0_c) @ L0_wmod).reshape(L0_c.shape[0], 6, 1, -1)
    sa, ca, ga, sb, cb, gb = (mod[:, 0], mod[:, 1], mod[:, 2], mod[:, 3], mod[:, 4], mod[:, 5])
    ga = (2 * (ga >= 0) - 1) * jnp.maximum(jnp.abs(ga), 0.25)
    gb = (2 * (gb >= 0) - 1) * jnp.maximum(jnp.abs(gb), 0.25)
    h = _layernorm(x, axis=-1) * (1 + ca) + sa
    x = x + ga * _L0_attn_ref(h, L0_attn_Wi, L0_attn_Wf, L0_attn_Wg, L0_attn_conv_i, L0_attn_conv_f, L0_attn_g_norm_weight, L0_attn_Wo)
    h = _layernorm(x, axis=-1) * (1 + cb) + sb
    x = x + gb * _L0_ffn_ref(h, L0_ffn_ln_gamma, L0_ffn_ln_beta, L0_ffn_gate_w, L0_ffn_w1, L0_ffn_w2)
    return x

_drawn_inputs = setup_inputs


def setup_inputs(seed=0):
    import zlib

    import numpy as np

    out = dict(_drawn_inputs(seed))
    spreads = {'L0_attn_g_norm_weight': (1.0, 0.2)}
    factors = {'L0_ffn_ln_gamma': 200.0, 'L0_ffn_ln_beta': 200.0}
    for name, (base, spread) in spreads.items():
        noise = np.random.default_rng([zlib.crc32(name.encode()), seed]).standard_normal(out[name].shape)
        drawn = base * np.exp(spread * noise) if base else spread * noise
        out[name] = jnp.asarray(drawn.astype(out[name].dtype))
    for name, factor in factors.items():
        out[name] = (out[name] * factor).astype(out[name].dtype)
    return out
```

```python
from contextlib import ExitStack

import numpy as np

import concourse.bass as bass
from concourse import mybir

F32, F16, I32, U32 = mybir.dt.float32, mybir.dt.float16, mybir.dt.int32, mybir.dt.uint32
ALU = mybir.AluOpType
ACT = mybir.ActivationFunctionType
AX = mybir.AxisListType

P = 128
B, T, C = 16, 512, 256
E, F = 8, 512
TAPS = 4
EPS = 1e-5
M = C // P
J = T // P
TILES = B * J
N = B * T
FC = F // P
BLK = 256
SUB = BLK // P
REGION = N + BLK
BLOCKS = 2 * N // BLK + E - 1
LOOP_BLOCKS = BLOCKS + BLOCKS % 2
ZW = TAPS - 1 + T
STAGE = 2048
ARENA = 16384
S = 64.0
S2 = S * S


class Count:

    def __init__(self, sem, per, lead=0):
        self.sem, self.per, self.lead = sem, per, lead

    def at(self, rnd, n=None):
        n = self.per if n is None else n
        return rnd * self.per + (self.lead * self.per + n)


def build(nc, x, wi, wf, wg, conv_i, conv_f, gnorm, wo, gamma, beta, gate, w1, w2, c_t, wmod, out):
    with ExitStack() as ctx:
        def sb(name, shape, dt=F32):
            return ctx.enter_context(nc.sbuf_tensor(name, shape, dt))

        def ps(name):
            return ctx.enter_context(nc.psum_tensor(name, [P, 512], F32))

        def sem(name):
            return ctx.enter_context(nc.semaphore(name))

        def count(name, per, lead=0):
            return Count(sem(name), per, lead)

        mod_rows = nc.dram_tensor("mod_rows", [B, 4 * C], F32, kind="Internal").ap()
        sorted_x = nc.dram_tensor("sorted_x", [E * REGION, C], F32, kind="Internal").ap()
        sorted_y = nc.dram_tensor("sorted_y", [LOOP_BLOCKS * BLK, C], F32, kind="Internal").ap()

        X = sb("X", [P, TILES, C])
        W1H = sb("W1H", [P, M * E * F], F16)
        W1L = sb("W1L", [P, M * E * F], F16)
        W2H = sb("W2H", [P, FC * E * C], F16)
        W2L = sb("W2L", [P, FC * E * C], F16)
        WPH = sb("WPH", [P, 3, M, C], F16)
        WPL = sb("WPL", [P, 3, M, C], F16)
        WOH = sb("WOH", [P, M, C], F16)
        WOL = sb("WOL", [P, M, C], F16)
        ident = sb("ident", [P, P])
        ones = sb("ones", [P, P])
        before = sb("before", [P, P], F16)
        ones16 = sb("ones16", [P, P], F16)
        expert_id = sb("expert_id", [P, E])
        minus_half = sb("minus_half", [P, J])
        conv = sb("conv", [P, 2, M, TAPS])
        h_scale = sb("h_scale", [P, M, B])
        bias = sb("bias", [P, 3, M, B])
        gate_c = sb("gate_c", [P, M, E])
        gate_b = sb("gate_b", [P, E])
        logits = sb("logits", [P, TILES, E])
        top = sb("top", [P, TILES, 8])
        slots = sb("slots", [P, B, 2 * J], I32)
        base = sb("base", [P, E])

        arena = sb("arena", [P, ARENA])

        def place(cursor, shape, dt=F32):
            n = int(np.prod(shape))
            words = n if dt != F16 else n // 2
            ap = arena[:, cursor[0]:cursor[0] + words]
            cursor[0] += words
            assert cursor[0] <= ARENA
            if dt != F32:
                ap = ap.bitcast(dt)
            if len(shape) == 2:
                ap = ap.rearrange("p (a b) -> p a b", b=shape[1])
            if len(shape) == 3:
                ap = ap.rearrange("p (a b c) -> p a b c", b=shape[1], c=shape[2])
            return ap

        bank = [ps(f"bank{n}") for n in range(8)]

        def flat(ap):
            return ap.rearrange("p a b -> p (a b)")

        at = [0]
        c_in = place(at, [M, B])
        silu_c = place(at, [M, B])
        shift_t = place(at, [M, B])
        w_mod = place(at, [M, 6 * C])
        w_in = place(at, [4, M * C])
        norm_w = place(at, [M])
        gamma_c = place(at, [M])
        beta_c = place(at, [M])
        gate_t = place(at, [M, E])
        gate_gb = place(at, [M, 2 * E])
        rows_sb = place(at, [4, C])[0:B]
        sign_sb = place(at, [2, C])[0:B]
        stage = [place(at, [STAGE]) for _ in range(2)]

        consts = sem("consts")
        small_in = sem("small_in")
        c_ok, mod_ok, mod_sb, bias_ok, bias_sb = map(sem, ("c_ok", "mod_ok", "mod_sb", "bias_ok", "bias_sb"))
        gate_ok, gate_in = sem("gate_ok"), sem("gate_in")
        rows_ok, rows_out = sem("rows_ok"), sem("rows_out")
        wo_ok, split_hi, split_lo = sem("wo_ok"), sem("split_hi"), sem("split_lo")
        stage_in = [sem("stage_in0"), sem("stage_in1")]
        setup_dve = sem("setup_dve")
        SMALL = 12
        CHUNKS = (M * E * F + FC * E * C) // STAGE
        w1_chunks = M * E * F // STAGE

        with nc.Block() as block:

            @block.sync
            def _(sp):
                loads = [
                    (c_in, c_t.rearrange("(k p) b -> p k b", p=P)),
                    (conv[:, 0], conv_f.rearrange("(m p) k -> p m k", p=P)),
                    (conv[:, 1], conv_i.rearrange("(m p) k -> p m k", p=P)),
                    (norm_w, gnorm),
                    (gamma_c, gamma),
                    (beta_c, beta),
                    (gate_t, gate.rearrange("(m p) e -> p m e", p=P)),
                    (w_mod, wmod.rearrange("(k p) n -> p k n", p=P)),
                ] + [(w_in[:, n].rearrange("p (k n) -> p k n", k=M), w.rearrange("(k p) n -> p k n", p=P))
                     for n, w in enumerate((wf, wi, wg, wo))]
                assert len(loads) == SMALL
                for dst, src in loads:
                    sp.dma_start(dst, src).then_inc(small_in, 16)
                for n in range(CHUNKS):
                    if n >= 2:
                        sp.wait_ge(split_lo, n - 1)
                    w, k = (w1, n) if n < w1_chunks else (w2, n - w1_chunks)
                    per = (E * F if w is w1 else E * C) // STAGE
                    src = w[(k // per) * P:(k // per + 1) * P, (k % per) * STAGE:(k % per + 1) * STAGE]
                    sp.dma_start(stage[n % 2], src).then_inc(stage_in[n % 2], 16)
                    if n == 2:
                        sp.wait_ge(rows_ok, 1)
                        sp.dma_start(mod_rows.rearrange("b (q c) -> b q c", q=4), rows_sb).then_inc(rows_out, 16)
                sp.wait_ge(rows_out, 16)

            @block.gpsimd
            def _(pool):
                nc.gpsimd.memset(ident[:], 0.0).then_inc(consts, 1)
                nc.gpsimd.memset(ones[:], 1.0).then_inc(consts, 1)
                nc.gpsimd.memset(ones16[:], 1.0).then_inc(consts, 1)
                nc.gpsimd.memset(minus_half[:], -0.5).then_inc(consts, 1)
                nc.gpsimd.iota(expert_id[:], pattern=[[1, E]], base=0, channel_multiplier=0,
                               allow_small_or_imprecise_dtypes=True).then_inc(consts, 1)
                nc.gpsimd.iota(base[:], pattern=[[REGION, E]], base=0, channel_multiplier=0,
                               allow_small_or_imprecise_dtypes=True).then_inc(consts, 1)
                pool.wait_ge(consts, 6)
                nc.gpsimd.affine_select(out=ident[:], in_=ident[:], compare_op=ALU.not_equal, fill=1.0,
                                        base=0, pattern=[[-1, P]], channel_multiplier=1).then_inc(consts, 1)
                nc.gpsimd.affine_select(out=before[:], in_=ones16[:], compare_op=ALU.is_gt, fill=0.0,
                                        base=0, pattern=[[1, P]], channel_multiplier=-1).then_inc(consts, 1)
                pool.wait_ge(consts, 8)

            @block.scalar
            def _(act):
                nc.scalar.preload_act_table(ACT.Silu)
                act.wait_ge(small_in, 16 * SMALL)
                nc.scalar.activation(silu_c, c_in, ACT.Silu).then_inc(c_ok, 1)
                for n in range(3):
                    nc.scalar.activation(flat(WPH[:, n]), w_in[:, n], ACT.Copy, scale=S).then_inc(split_hi, 1)
                act.wait_ge(wo_ok, M)
                nc.scalar.activation(flat(WOH[:]), w_in[:, 3], ACT.Copy).then_inc(split_hi, 1)
                for n in range(CHUNKS):
                    act.wait_ge(stage_in[n % 2], 16 * (n // 2 + 1))
                    wh, k = (W1H, n) if n < w1_chunks else (W2H, n - w1_chunks)
                    nc.scalar.activation(wh[:, k * STAGE:(k + 1) * STAGE], stage[n % 2], ACT.Copy,
                                         scale=S).then_inc(split_hi, 1)

            @block.tensor
            def _(pe):
                pe.wait_ge(c_ok, 1)
                for q in range(2):
                    for k in range(M):
                        nc.tensor.matmul(bank[q][0:B, :], silu_c[:, k], 
                                         w_mod[:, k, (1 + q) * 2 * C:(2 + q) * 2 * C], start=k == 0, stop=k == M - 1).then_inc(mod_ok, 1)
                for q in range(2 * M):
                    for k in range(M):
                        nc.tensor.matmul(bank[2][:, q * B:(q + 1) * B], w_mod[:, k, q * P:(q + 1) * P],
                                         silu_c[:, k], start=k == 0, stop=k == M - 1).then_inc(mod_ok, 1)
                pe.wait_ge(mod_sb, 2)
                for n in range(3 * M):
                    p, m = divmod(n, M)
                    for k in range(M):
                        nc.tensor.matmul(bank[3][:, n * B:(n + 1) * B], w_in[:, p, k * C + m * P:k * C + (m + 1) * P],
                                         shift_t[:, k], start=k == 0, stop=k == M - 1).then_inc(bias_ok, 1)
                pe.wait_ge(gate_in, 2 * M)
                pe.wait_ge(consts, 8)
                for k in range(M):
                    nc.tensor.matmul(bank[4][:, 0:2 * E], ones[:], gate_gb[:, k], start=k == 0,
                                     stop=k == M - 1).then_inc(gate_ok, 1)

            @block.vector
            def _(dve):
                step = [0]

                def link(ins):
                    step[0] += 1
                    ins.then_inc(setup_dve, 1)
                    dve.wait_ge(setup_dve, step[0])

                dve.wait_ge(small_in, 16 * SMALL)
                for k in range(M):
                    nc.vector.tensor_scalar(gate_gb[:, k, 0:E], gate_t[:, k], gamma_c[:, k:k + 1], None,
                                            ALU.mult).then_inc(gate_in, 1)
                    nc.vector.tensor_scalar(gate_gb[:, k, E:2 * E], gate_t[:, k], beta_c[:, k:k + 1], None,
                                            ALU.mult).then_inc(gate_in, 1)
                for k in range(M):
                    nc.vector.tensor_scalar(w_in[:, 3, k * C:(k + 1) * C], w_in[:, 3, k * C:(k + 1) * C],
                                            norm_w[:, k:k + 1], -0.5 * S, ALU.mult, ALU.mult).then_inc(wo_ok, 1)
                dve.wait_ge(mod_ok, 2 * M + 2 * M * M)
                nc.vector.tensor_copy(flat(shift_t), bank[2][:, 0:M * B]).then_inc(mod_sb, 1)
                nc.vector.tensor_scalar(flat(h_scale[:]), bank[2][:, M * B:2 * M * B], 1.0, S, ALU.add,
                                        ALU.mult).then_inc(mod_sb, 1)
                for q, r, z in ((0, 0, 0), (1, 3, C)):
                    gain = bank[q][0:B, z:z + C]
                    link(nc.vector.tensor_scalar(sign_sb[:, 0], gain, 0.0, 2.0, ALU.is_ge, ALU.mult))
                    link(nc.vector.tensor_scalar(sign_sb[:, 1], gain, -1.0, 0.25, ALU.mult, ALU.max))
                    link(nc.vector.tensor_tensor(sign_sb[:, 1], sign_sb[:, 1], gain, ALU.max))
                    link(nc.vector.scalar_tensor_tensor(rows_sb[:, r], sign_sb[:, 0], -1.0, sign_sb[:, 1],
                                                        ALU.add, ALU.mult))
                link(nc.vector.tensor_copy(rows_sb[:, 1], bank[0][0:B, C:2 * C]))
                nc.vector.tensor_scalar(rows_sb[:, 2], bank[1][0:B, 0:C], 1.0, None, ALU.add).then_inc(rows_ok, 1)
                dve.wait_ge(bias_ok, 3 * M * M)
                nc.vector.tensor_copy(bias[:].rearrange("p a b c -> p (a b c)"),
                                      bank[3][:, 0:3 * M * B]).then_inc(bias_sb, 1)
                dve.wait_ge(gate_ok, M)
                dve.wait_ge(gate_in, 2 * M)
                nc.vector.tensor_copy(gate_b[:], bank[4][:, E:2 * E]).then_inc(bias_sb, 1)
                for k in range(M):
                    nc.vector.scalar_tensor_tensor(gate_c[:, k], bank[4][:, 0:E], -1.0 / C, gate_gb[:, k, 0:E],
                                                   ALU.mult, ALU.add).then_inc(bias_sb, 1)
                dve.wait_ge(split_hi, 3)
                for n in range(3):
                    nc.vector.scalar_tensor_tensor(flat(WPL[:, n]), w_in[:, n], S, flat(WPH[:, n]), ALU.mult,
                                                   ALU.subtract).then_inc(bias_sb, 1)
                dve.wait_ge(split_hi, 4)
                dve.wait_ge(wo_ok, M)
                nc.vector.tensor_tensor(flat(WOL[:]), w_in[:, 3], flat(WOH[:]), ALU.subtract).then_inc(bias_sb, 1)
                for n in range(CHUNKS):
                    dve.wait_ge(split_hi, 5 + n)
                    dve.wait_ge(stage_in[n % 2], 16 * (n // 2 + 1))
                    (wh, wl), k = ((W1H, W1L), n) if n < w1_chunks else ((W2H, W2L), n - w1_chunks)
                    cols = slice(k * STAGE, (k + 1) * STAGE)
                    nc.vector.scalar_tensor_tensor(wl[:, cols], stage[n % 2], S, wh[:, cols], ALU.mult,
                                                   ALU.subtract).then_inc(split_lo, 1)

        at = [0]
        xn = place(at, [J, C])
        hh, hl = place(at, [M, T], F16), place(at, [M, T], F16)
        z = place(at, [2, M, ZW])
        y = place(at, [2, M, T])
        sg = place(at, [M, T])
        th = place(at, [M, T])
        si = place(at, [M, T])
        h = place(at, [M, T])
        sq = place(at, [M, T])
        attn = flat(sq).rearrange("p (j c) -> p j c", c=C)
        uh, ul = place(at, [M, T], F16), place(at, [M, T], F16)
        mod_b = place(at, [3, C])
        h2 = place(at, [J, C])
        h2_tsb = place(at, [M, T])
        bns1, bns2 = place(at, [J, 6]), place(at, [J, 6])
        mv1, mv2, mv3 = place(at, [J, 2]), place(at, [J, 2]), place(at, [J, 2])
        r1, r2, r3, rms = (place(at, [J]) for _ in range(4))
        v1, v2, v3, v4 = (place(at, [J]) for _ in range(4))
        picks = place(at, [J, 8], U32)
        picks_f = place(at, [2, J])
        hot = place(at, [2 * J, E])
        ranked_hot = place(at, [2 * J, E])
        hot2 = place(at, [J, E], F16)
        rank = place(at, [J, E])
        logit_b, top_b = place(at, [J, E]), place(at, [J, E])
        slots_f = place(at, [2 * J])
        slots_b = place(at, [2 * J], I32)
        tpa, prj, opj = bank[0:2], bank[2:4], bank[4:6]
        ssq_bank, route_bank = bank[6], bank[7]
        ssq = ssq_bank[:, 0:J]
        score = route_bank[:, 0:J * E]
        ahead = route_bank[:, J * E:2 * J * E]
        total = route_bank[:, 2 * J * E:2 * J * E + E]

        pads = sem("pads")
        dve_settled, pool_settled = sem("dve_settled"), sem("pool_settled")
        x_in = count("x_in", 16)
        mod_in = count("mod_in", 16)
        stats1, moments1 = count("stats1", J), count("moments1", J)
        var1, rstd1 = count("var1", 1), count("rstd1", 1)
        normed = count("normed", J)
        xn_t = count("xn_t", M, 1)
        h_hi, h_lo = count("h_hi", M), count("h_lo", M, 1)
        projected = count("projected", 6, 1)
        evac = count("evac", 6, 1)
        y0_ok = count("y0_ok", 2 * M)
        conv_ok = count("conv_ok", 2 * M * (TAPS - 1), 1)
        act_ok = count("act_ok", 2 * M, 1)
        gate_i, gate_f = count("gate_i", M), count("gate_f", M)
        scanned = count("scanned", M, 1)
        sq_ok = count("sq_ok", M, 1)
        ssq_ok, rms_in, rms_ok = count("ssq_ok", 1), count("rms_in", 1, 1), count("rms_ok", 1)
        u_ok, u_hi, u_lo = count("u_ok", M), count("u_hi", M), count("u_lo", M, 1)
        o_ok = count("o_ok", 2, 1)
        attn_ok = count("attn_ok", J)
        x1_ok = count("x1_ok", 1, 1)
        stats2, moments2 = count("stats2", J), count("moments2", J)
        var2, rstd2 = count("var2", 1), count("rstd2", 1)
        scaled2, h2_ok = count("scaled2", J), count("h2_ok", J, 1)
        stats3, moments3 = count("stats3", J), count("moments3", J)
        var3, rstd3 = count("var3", 1), count("rstd3", 1)
        h2_t, h2_sb = count("h2_t", M), count("h2_sb", M, 1)
        scored, score_in = count("scored", 1), count("score_in", J, 1)
        top_ok, picked, pick_f = count("top_ok", J), count("picked", J), count("pick_f", 2)
        kept = count("kept", 2)
        hot_ok, hot2_ok = count("hot_ok", 2), count("hot2_ok", 1)
        counted, rank_ok, base_ok = count("counted", 1), count("rank_ok", 1), count("base_ok", 1)
        own_rank, slot_f, slot_ok = count("own_rank", 2), count("slot_f", 1), count("slot_ok", 2)
        scattered = count("scattered", 16 * 2 * J)
        rows_free = count("rows_free", 1, 1)

        with nc.Block() as block:

            @block.sync
            def _(sp):
                sp.sem_inc(rows_free.sem, 1)
                with sp.Fori(0, B) as b:
                    sp.dma_start(X[:, bass.ds(b * J, J), :],
                                 x[bass.ds(b * T, T), :].rearrange("(j p) c -> p j c", p=P)).then_inc(x_in.sem, 16)
                    sp.wait_ge(h2_ok.sem, h2_ok.at(b - 1))
                    sp.dma_start(mod_b.rearrange("p q c -> p (q c)"),
                                 mod_rows[bass.ds(b, 1), 0:3 * C].to_broadcast([P, 3 * C])).then_inc(mod_in.sem, 16)
                    sp.wait_ge(x_in.sem, x_in.at(b))
                    sp.wait_ge(mod_in.sem, mod_in.at(b))
                    sp.wait_ge(scattered.sem, scattered.at(b))
                    sp.sem_inc(rows_free.sem, 1)

            @block.gpsimd
            def _(pool):
                def settle():
                    pool.sem_inc(pool_settled, 1)

                def rstd(b, moments, n, mv, v, var, r, ok, scale=1.0):
                    pool.wait_ge(moments.sem, moments.at(b, n))
                    settle()
                    nc.gpsimd.tensor_scalar(v, mv[:, :, 1], EPS, None, ALU.add).then_inc(var.sem, 1)
                    pool.wait_ge(var.sem, var.at(b))
                    nc.gpsimd.tensor_tensor(r, v, minus_half[:], ALU.pow).then_inc(ok.sem, 1)

                pool.sem_inc(x1_ok.sem, 1)
                with pool.Fori(0, B) as b:
                    rstd(b, moments1, J, mv1, v1, var1, r1, rstd1)
                    for n in range(2 * M):
                        p, m = divmod(n, M)
                        pool.wait_ge(evac.sem, evac.at(b, n + 1))
                        pool.wait_ge(act_ok.sem, act_ok.at(b - 1, n + 1))
                        settle()
                        nc.gpsimd.tensor_scalar(y[:, p, m], z[:, p, m, ZW - T:ZW], conv[:, p, m, TAPS - 1:TAPS], None,
                                                ALU.mult).then_inc(y0_ok.sem, 1)
                    pool.wait_ge(rms_in.sem, rms_in.at(b))
                    nc.gpsimd.tensor_tensor(rms, v4, minus_half[:], ALU.pow).then_inc(rms_ok.sem, 1)
                    pool.wait_ge(attn_ok.sem, attn_ok.at(b))
                    xb = X[:, bass.ds(b * J, J), :]
                    nc.gpsimd.tensor_tensor(xb, xb, attn, ALU.add).then_inc(x1_ok.sem, 1)
                    rstd(b, moments2, J, mv2, v2, var2, r2, rstd2)
                    rstd(b, moments3, J, mv3, v3, var3, r3, rstd3)
                    pool.wait_ge(slot_ok.sem, slot_ok.at(b, 1))
                    settle()
                    for n in range(2 * J):
                        pool.indirect_dma_start(sorted_x, bass.IndirectOffsetOnAxis(ap=slots_b[:, n:n + 1], axis=0),
                                                h2[:, n % J], None).then_inc(scattered.sem, 16)

            @block.scalar
            def _(act):
                act.sem_inc(evac.sem, 6)
                act.sem_inc(act_ok.sem, 2 * M)
                act.sem_inc(sq_ok.sem, M)
                act.sem_inc(h2_sb.sem, M)
                nc.scalar.preload_act_table(ACT.Silu)
                with act.Fori(0, B) as b:
                    for m in range(M):
                        act.wait_ge(xn_t.sem, xn_t.at(b, m + 1))
                        act.wait_ge(projected.sem, projected.at(b - 1))
                        nc.scalar.activation(hh[:, m], tpa[m][:], ACT.Copy,
                                             scale=h_scale[:, m, bass.ds(b, 1)]).then_inc(h_hi.sem, 1)
                    for n in range(6):
                        p, m = divmod(n, M)
                        act.wait_ge(projected.sem, projected.at(b, n + 1))
                        if p < 2:
                            act.wait_ge(conv_ok.sem, conv_ok.at(b - 1))
                            nc.scalar.activation(z[:, p, m, ZW - T:ZW], prj[n % 2][:], ACT.Identity, scale=1 / S2,
                                                 bias=bias[:, p, m, bass.ds(b, 1)]).then_inc(evac.sem, 1)
                        else:
                            act.wait_ge(u_lo.sem, u_lo.at(b - 1))
                            nc.scalar.activation(sg[:, m], prj[n % 2][:], ACT.Silu, scale=1 / S2,
                                                 bias=bias[:, p, m, bass.ds(b, 1)]).then_inc(evac.sem, 1)
                    last = 2 * M * (TAPS - 2)
                    for n in range(2 * M):
                        p, m = divmod(n, M)
                        act.wait_ge(conv_ok.sem, conv_ok.at(b, last + n + 1))
                        act.wait_ge(scanned.sem, scanned.at(b - 1, m + 1))
                        if p == 0:
                            nc.scalar.activation(th[:, m], y[:, 0, m], ACT.Tanh, scale=0.5).then_inc(act_ok.sem, 1)
                        else:
                            nc.scalar.activation(si[:, m], y[:, 1, m], ACT.Silu).then_inc(act_ok.sem, 1)
                    for m in range(M):
                        act.wait_ge(scanned.sem, scanned.at(b, m + 1))
                        act.wait_ge(x1_ok.sem, x1_ok.at(b - 1))
                        nc.scalar.activation(sq[:, m], h[:, m], ACT.Square).then_inc(sq_ok.sem, 1)
                    for m in range(M):
                        act.wait_ge(u_ok.sem, u_ok.at(b, m + 1))
                        act.wait_ge(o_ok.sem, o_ok.at(b - 1))
                        nc.scalar.activation(uh[:, m], sg[:, m], ACT.Copy, scale=S).then_inc(u_hi.sem, 1)
                    for m in range(M):
                        act.wait_ge(h2_t.sem, h2_t.at(b, m + 1))
                        nc.scalar.activation(h2_tsb[:, m], opj[m][:], ACT.Copy).then_inc(h2_sb.sem, 1)

            @block.vector
            def _(dve):
                dve.sem_inc(h_lo.sem, M)
                dve.sem_inc(conv_ok.sem, conv_ok.per)
                dve.sem_inc(scanned.sem, M)
                dve.sem_inc(rms_in.sem, 1)
                dve.sem_inc(u_lo.sem, M)
                dve.sem_inc(h2_ok.sem, J)
                dve.sem_inc(score_in.sem, J)
                for p in range(2):
                    nc.vector.memset(z[:, p, :, 0:ZW - T], 0.0).then_inc(pads, 1)
                dve.wait_ge(pads, 2)
                def settle():
                    dve.sem_inc(dve_settled, 1)

                with dve.Fori(0, B) as b:
                    dve.wait_ge(x_in.sem, x_in.at(b))
                    settle()
                    for j in range(J):
                        nc.vector.bn_stats(bns1[:, j], flat(X[:, bass.ds(b * J + j, 1), :])).then_inc(stats1.sem, 1)
                    for j in range(J):
                        dve.wait_ge(stats1.sem, stats1.at(b, j + 1))
                        settle()
                        nc.vector.bn_aggr(mv1[:, j], bns1[:, j]).then_inc(moments1.sem, 1)
                    dve.wait_ge(rstd1.sem, rstd1.at(b))
                    dve.wait_ge(xn_t.sem, xn_t.at(b - 1))
                    for j in range(J):
                        nc.vector.tensor_scalar(xn[:, j], flat(X[:, bass.ds(b * J + j, 1), :]), mv1[:, j, 0:1],
                                                r1[:, j:j + 1], ALU.subtract, ALU.mult).then_inc(normed.sem, 1)
                    for m in range(M):
                        dve.wait_ge(h_hi.sem, h_hi.at(b, m + 1))
                        dve.wait_ge(projected.sem, projected.at(b - 1))
                        nc.vector.scalar_tensor_tensor(hl[:, m], tpa[m][:], h_scale[:, m, bass.ds(b, 1)], hh[:, m],
                                                       ALU.mult, ALU.subtract).then_inc(h_lo.sem, 1)
                    for k in range(1, TAPS):
                        for n in range(2 * M):
                            p, m = divmod(n, M)
                            if k == 1:
                                dve.wait_ge(y0_ok.sem, y0_ok.at(b, n + 1))
                            else:
                                dve.wait_ge(conv_ok.sem, conv_ok.at(b, (k - 2) * 2 * M + n + 1))
                            nc.vector.scalar_tensor_tensor(
                                y[:, p, m], z[:, p, m, ZW - T - k:ZW - k], conv[:, p, m, TAPS - 1 - k:TAPS - k],
                                y[:, p, m], ALU.mult, ALU.add).then_inc(conv_ok.sem, 1)
                    for m in range(M):
                        dve.wait_ge(act_ok.sem, act_ok.at(b, M + m + 1))
                        nc.vector.scalar_tensor_tensor(si[:, m], th[:, m], -1.0, si[:, m], ALU.add,
                                                       ALU.mult).then_inc(gate_i.sem, 1)
                    for m in range(M):
                        dve.wait_ge(gate_i.sem, gate_i.at(b, m + 1))
                        nc.vector.tensor_scalar(th[:, m], th[:, m], 0.5, 0.5, ALU.mult,
                                                ALU.add).then_inc(gate_f.sem, 1)
                    for m in range(M):
                        dve.wait_ge(gate_f.sem, gate_f.at(b, m + 1))
                        dve.wait_ge(sq_ok.sem, sq_ok.at(b - 1, m + 1))
                        nc.vector.tensor_tensor_scan(h[:, m], th[:, m], si[:, m], 0.0, ALU.mult,
                                                     ALU.add).then_inc(scanned.sem, 1)
                    for m in range(M):
                        dve.wait_ge(scanned.sem, scanned.at(b, m + 1))
                        dve.wait_ge(evac.sem, evac.at(b, 4 + m + 1))
                        nc.vector.tensor_tensor(sg[:, m], sg[:, m], h[:, m], ALU.mult).then_inc(u_ok.sem, 1)
                    dve.wait_ge(ssq_ok.sem, ssq_ok.at(b))
                    nc.vector.tensor_scalar(v4, ssq, S2 * S2 / (4 * C), S2 * S2 * EPS, ALU.mult,
                                            ALU.add).then_inc(rms_in.sem, 1)
                    for m in range(M):
                        dve.wait_ge(u_hi.sem, u_hi.at(b, m + 1))
                        dve.wait_ge(o_ok.sem, o_ok.at(b - 1))
                        nc.vector.scalar_tensor_tensor(ul[:, m], sg[:, m], S, uh[:, m], ALU.mult,
                                                       ALU.subtract).then_inc(u_lo.sem, 1)
                    dve.wait_ge(rms_ok.sem, rms_ok.at(b))
                    dve.wait_ge(mod_in.sem, mod_in.at(b))
                    for j in range(J):
                        dve.wait_ge(o_ok.sem, o_ok.at(b, j // 2 + 1))
                        nc.vector.scalar_tensor_tensor(attn[:, j], opj[j // 2][:, (j % 2) * C:(j % 2 + 1) * C],
                                                       rms[:, j:j + 1], mod_b[:, 0], ALU.mult,
                                                       ALU.mult).then_inc(attn_ok.sem, 1)
                    dve.wait_ge(x1_ok.sem, x1_ok.at(b))
                    settle()
                    for j in range(J):
                        nc.vector.bn_stats(bns2[:, j], flat(X[:, bass.ds(b * J + j, 1), :])).then_inc(stats2.sem, 1)
                    for j in range(J):
                        dve.wait_ge(stats2.sem, stats2.at(b, j + 1))
                        settle()
                        nc.vector.bn_aggr(mv2[:, j], bns2[:, j]).then_inc(moments2.sem, 1)
                    dve.wait_ge(moments2.sem, moments2.at(b))
                    dve.wait_ge(rows_free.sem, rows_free.at(b - 1))
                    dve.wait_ge(h2_sb.sem, h2_sb.at(b - 1))
                    for j in range(J):
                        nc.vector.scalar_tensor_tensor(h2[:, j], flat(X[:, bass.ds(b * J + j, 1), :]), mv2[:, j, 0:1],
                                                       mod_b[:, 2], ALU.subtract, ALU.mult).then_inc(scaled2.sem, 1)
                    dve.wait_ge(rstd2.sem, rstd2.at(b))
                    for j in range(J):
                        dve.wait_ge(scaled2.sem, scaled2.at(b, j + 1))
                        nc.vector.scalar_tensor_tensor(h2[:, j], h2[:, j], r2[:, j:j + 1], mod_b[:, 1], ALU.mult,
                                                       ALU.add).then_inc(h2_ok.sem, 1)
                    for j in range(J):
                        dve.wait_ge(h2_ok.sem, h2_ok.at(b, j + 1))
                        nc.vector.bn_stats(bns2[:, j], h2[:, j]).then_inc(stats3.sem, 1)
                    for j in range(J):
                        dve.wait_ge(stats3.sem, stats3.at(b, j + 1))
                        settle()
                        nc.vector.bn_aggr(mv3[:, j], bns2[:, j]).then_inc(moments3.sem, 1)
                    dve.wait_ge(rstd3.sem, rstd3.at(b))
                    dve.wait_ge(scored.sem, scored.at(b))
                    for j in range(J):
                        nc.vector.scalar_tensor_tensor(
                            logit_b[:, j], score[:, j * E:(j + 1) * E], r3[:, j:j + 1],
                            gate_b[:], ALU.mult, ALU.add).then_inc(score_in.sem, 1)
                    for j in range(J):
                        dve.wait_ge(score_in.sem, score_in.at(b, j + 1))
                        settle()
                        nc.vector.max(top_b[:, j], logit_b[:, j]).then_inc(top_ok.sem, 1)
                    for j in range(J):
                        dve.wait_ge(top_ok.sem, top_ok.at(b, j + 1))
                        settle()
                        nc.vector.max_index(picks[:, j], top_b[:, j], logit_b[:, j]).then_inc(picked.sem, 1)
                    nc.vector.tensor_copy(logits[:, bass.ds(b * J, J), :], logit_b).then_inc(kept.sem, 1)
                    nc.vector.tensor_copy(top[:, bass.ds(b * J, J), :], top_b).then_inc(kept.sem, 1)
                    dve.wait_ge(picked.sem, picked.at(b))
                    for n in range(2):
                        nc.vector.tensor_copy(picks_f[:, n], picks[:, :, n]).then_inc(pick_f.sem, 1)
                    for n in range(2):
                        dve.wait_ge(pick_f.sem, pick_f.at(b, n + 1))
                        nc.vector.tensor_tensor(
                            hot[:, n * J:(n + 1) * J], expert_id[:].unsqueeze(1).to_broadcast([P, J, E]),
                            picks_f[:, n].unsqueeze(2).to_broadcast([P, J, E]), ALU.is_equal).then_inc(hot_ok.sem, 1)
                    dve.wait_ge(hot_ok.sem, hot_ok.at(b))
                    nc.vector.tensor_tensor(hot2, hot[:, 0:J], hot[:, J:2 * J], ALU.add).then_inc(hot2_ok.sem, 1)
                    dve.wait_ge(counted.sem, counted.at(b))
                    nc.vector.tensor_tensor(rank, ahead.rearrange("p (j e) -> p j e", e=E),
                                            base[:].unsqueeze(1).to_broadcast([P, J, E]),
                                            ALU.add).then_inc(rank_ok.sem, 1)
                    dve.wait_ge(rank_ok.sem, rank_ok.at(b))
                    nc.vector.tensor_tensor(base[:], base[:], total, ALU.add).then_inc(base_ok.sem, 1)
                    for n in range(2):
                        nc.vector.tensor_tensor(ranked_hot[:, n * J:(n + 1) * J], hot[:, n * J:(n + 1) * J], rank,
                                                ALU.mult).then_inc(own_rank.sem, 1)
                    dve.wait_ge(own_rank.sem, own_rank.at(b))
                    nc.vector.tensor_reduce(slots_f, ranked_hot, AX.X, ALU.add).then_inc(slot_f.sem, 1)
                    dve.wait_ge(slot_f.sem, slot_f.at(b))
                    nc.vector.tensor_copy(slots_b, slots_f).then_inc(slot_ok.sem, 1)
                    nc.vector.tensor_copy(flat(slots[:, bass.ds(b, 1), :]), slots_f).then_inc(slot_ok.sem, 1)

            @block.tensor
            def _(pe):
                pe.sem_inc(xn_t.sem, M)
                pe.sem_inc(projected.sem, 6)
                pe.sem_inc(o_ok.sem, 2)

                with pe.Fori(0, B) as b:
                    for m in range(M):
                        pe.wait_ge(h_lo.sem, h_lo.at(b - 1, m + 1))
                        for j in range(J):
                            pe.wait_ge(normed.sem, normed.at(b, j + 1))
                            last = nc.tensor.transpose(tpa[m][:, j * P:(j + 1) * P], xn[:, j, m * P:(m + 1) * P],
                                                       ident[:])
                        last.then_inc(xn_t.sem, 1)
                    pe.wait_ge(h_lo.sem, h_lo.at(b))
                    for n in range(6):
                        p, m = divmod(n, M)
                        cols = slice(m * P, (m + 1) * P)
                        pe.wait_ge(evac.sem, evac.at(b, n - 1) if n >= 2 else evac.at(b - 1, n + 5))
                        for k in range(M):
                            nc.tensor.matmul(prj[n % 2][:], WPH[:, p, k, cols], hh[:, k], start=k == 0, stop=False)
                            nc.tensor.matmul(prj[n % 2][:], WPH[:, p, k, cols], hl[:, k], start=False, stop=False)
                            last = nc.tensor.matmul(prj[n % 2][:], WPL[:, p, k, cols], hh[:, k], start=False,
                                                    stop=k == M - 1)
                        last.then_inc(projected.sem, 1)
                    pe.wait_ge(rms_in.sem, rms_in.at(b - 1))
                    pe.wait_ge(sq_ok.sem, sq_ok.at(b))
                    for j in range(J):
                        for m in range(M):
                            last = nc.tensor.matmul(ssq[:, j:j + 1], sq[:, m, j * P:(j + 1) * P], ones[:, 0:1],
                                                    start=m == 0, stop=m == M - 1)
                    last.then_inc(ssq_ok.sem, 1)
                    pe.wait_ge(h2_sb.sem, h2_sb.at(b - 1))
                    pe.wait_ge(u_lo.sem, u_lo.at(b))
                    for j in range(J):
                        dst = opj[j // 2][:, (j % 2) * C:(j % 2 + 1) * C]
                        tok = slice(j * P, (j + 1) * P)
                        for m in range(M):
                            nc.tensor.matmul(dst, uh[:, m, tok], WOH[:, m], start=m == 0, stop=False)
                            nc.tensor.matmul(dst, uh[:, m, tok], WOL[:, m], start=False, stop=False)
                            last = nc.tensor.matmul(dst, ul[:, m, tok], WOH[:, m], start=False, stop=m == M - 1)
                        if j % 2:
                            last.then_inc(o_ok.sem, 1)
                    for m in range(M):
                        for j in range(J):
                            pe.wait_ge(h2_ok.sem, h2_ok.at(b, j + 1))
                            last = nc.tensor.transpose(opj[m][:, j * P:(j + 1) * P], h2[:, j, m * P:(m + 1) * P],
                                                       ident[:])
                        last.then_inc(h2_t.sem, 1)
                    pe.wait_ge(h2_sb.sem, h2_sb.at(b))
                    for j in range(J):
                        for m in range(M):
                            last = nc.tensor.matmul(score[:, j * E:(j + 1) * E], h2_tsb[:, m, j * P:(j + 1) * P],
                                                    gate_c[:, m], start=m == 0, stop=m == M - 1)
                    last.then_inc(scored.sem, 1)
                    pe.wait_ge(hot2_ok.sem, hot2_ok.at(b))
                    pe.wait_ge(score_in.sem, score_in.at(b))
                    for j in range(J):
                        for i in range(j + 1):
                            nc.tensor.matmul(ahead[:, j * E:(j + 1) * E], (before if i == j else ones16)[:],
                                             hot2[:, i], start=i == 0, stop=i == j)
                    for j in range(J):
                        last = nc.tensor.matmul(total, ones16[:], hot2[:, j], start=j == 0, stop=j == J - 1)
                    last.then_inc(counted.sem, 1)

        at = [0]
        zeros = place(at, [SUB, C])
        spread = place(at, [TILES, E])
        ratio = place(at, [TILES])
        denom = place(at, [TILES])
        prob = sb("prob", [P, 2, TILES])
        table = [place(at, [LOOP_BLOCKS])[0:1] for _ in range(5)]
        number, inner, row, pick, extra = table
        cnt, nblk, cum, jump, rounded = (place(at, [E]) for _ in range(5))
        cnt_i = place(at, [E], I32)
        slot_y, past = place(at, [B * 2 * J]), place(at, [B * 2 * J])
        free_i = place(at, [E], I32)[0:1]
        from_row, which = (place(at, [LOOP_BLOCKS], I32)[0:1] for _ in range(2))
        xin = [place(at, [SUB, C]) for _ in range(2)]
        xh = [place(at, [M, BLK], F16) for _ in range(2)]
        xl = [place(at, [M, BLK], F16) for _ in range(2)]
        gel = [place(at, [FC, BLK]) for _ in range(2)]
        gh = [place(at, [FC, BLK], F16) for _ in range(2)]
        gl = [place(at, [FC, BLK], F16) for _ in range(2)]
        yo = [place(at, [SUB, C]) for _ in range(2)]
        xt_bank, y_bank = bank[0:2], bank[2:4]
        hid = [bank[4:6], bank[6:8]]

        iotas, table_dve, table_ok = sem("iotas"), sem("table_dve"), sem("table_ok")
        spread_ok, exp_ok = sem("spread_ok"), sem("exp_ok")
        padded = sem("padded")
        rows_in = [count(f"rows_in{s}", 16) for s in range(2)]
        y_out = [count(f"y_out{s}", 16) for s in range(2)]
        rows_t = count("rows_t", 1, 2)
        x_hi, x_lo = count("x_hi", 1, 2), count("x_lo", 1, 2)
        hid_ok = count("hid_ok", 2, 2)
        gelu_ok = count("gelu_ok", 2, 2)
        g_hi, g_lo = count("g_hi", 2, 2), count("g_lo", 2, 2)
        y_ok, y_sb = count("y_ok", 1, 2), count("y_sb", 1, 2)
        HALF = LOOP_BLOCKS // 2 - 1

        def pairs(eng, first, body, last):
            first()
            with eng.Fori(0, HALF) as q:
                body(q, 1)
                body(q, 2)
            last()

        with nc.Block() as block:

            @block.gpsimd
            def _(pool):
                nc.gpsimd.iota(number, pattern=[[1, LOOP_BLOCKS]], base=0, channel_multiplier=0,
                               allow_small_or_imprecise_dtypes=True).then_inc(iotas, 1)
                nc.gpsimd.memset(zeros, 0.0).then_inc(iotas, 1)

            @block.sync
            def _(sp):
                sp.wait_ge(table_ok, 3)
                sp.wait_ge(iotas, 2)
                for e in range(E):
                    first = sp.value_load(free_i[0:1, e:e + 1], min_val=0, max_val=E * REGION - BLK)
                    sp.dma_start(sorted_x[bass.ds(first, BLK), :].rearrange("(s p) c -> p s c", p=P),
                                 zeros).then_inc(padded, 16)
                sp.wait_ge(padded, 16 * E)

                def load(q, k):
                    sp.wait_ge(rows_t.sem, rows_t.at(2 * q + k - 2))
                    first = sp.value_load(from_row[0:1, bass.ds(2 * q + k, 1)], min_val=0, max_val=E * REGION - BLK)
                    sp.dma_start(xin[k % 2], sorted_x[bass.ds(first, BLK), :].rearrange("(s p) c -> p s c", p=P)
                                 ).then_inc(rows_in[k % 2].sem, 16)

                def store(q, k):
                    sp.wait_ge(y_sb.sem, y_sb.at(2 * q + k))
                    sp.dma_start(sorted_y[bass.ds((2 * q + k) * BLK, BLK), :].rearrange("(s p) c -> p s c", p=P), yo[k % 2]
                                 ).then_inc(y_out[k % 2].sem, 16)

                load(0, 0)
                load(0, 1)
                with sp.Fori(0, HALF) as q:
                    for k in (1, 2):
                        load(q, k + 1)
                        store(q, k - 1)
                store(HALF, 0)
                store(HALF, 1)
                for s in range(2):
                    sp.wait_ge(y_out[s].sem, 16 * LOOP_BLOCKS // 2)

            @block.scalar
            def _(act):
                act.sem_inc(x_hi.sem, 2)
                act.sem_inc(gelu_ok.sem, 4)
                act.sem_inc(y_sb.sem, 2)
                act.wait_ge(spread_ok, 2)
                nc.scalar.activation(flat(spread), flat(spread), ACT.Exp).then_inc(exp_ok, 1)
                nc.scalar.activation(ratio, ratio, ACT.Exp).then_inc(exp_ok, 1)
                nc.scalar.preload_act_table(ACT.Gelu)

                def high(q, k):
                    act.wait_ge(rows_t.sem, rows_t.at(2 * q + k))
                    act.wait_ge(hid_ok.sem, hid_ok.at(2 * q + k - 2))
                    nc.scalar.activation(flat(xh[k % 2]), xt_bank[k % 2][:], ACT.Copy, scale=S).then_inc(x_hi.sem, 1)

                def gelu(q, k):
                    for n in range(2):
                        act.wait_ge(hid_ok.sem, hid_ok.at(2 * q + k, n + 1))
                        act.wait_ge(g_lo.sem, g_lo.at(2 * q + k - 2))
                        nc.scalar.activation(flat(gel[k % 2][:, 2 * n:2 * n + 2]), hid[k % 2][n][:], ACT.Gelu,
                                             scale=1 / S2).then_inc(gelu_ok.sem, 1)

                def evacuate(q, k, reuse=True):
                    act.wait_ge(y_ok.sem, y_ok.at(2 * q + k))
                    if reuse:
                        act.wait_ge(y_out[k % 2].sem, y_out[k % 2].at(q + k // 2 - 1))
                    nc.scalar.activation(flat(yo[k % 2]), y_bank[k % 2][:], ACT.Copy, scale=1 / S2).then_inc(y_sb.sem, 1)

                high(0, 0)
                high(0, 1)
                gelu(0, 0)
                high(0, 2)
                gelu(0, 1)
                evacuate(0, 0, False)
                high(0, 3)
                gelu(0, 2)
                evacuate(0, 1, False)
                with act.Fori(1, HALF) as q:
                    for k in (1, 2):
                        high(q, k + 1)
                        gelu(q, k)
                        evacuate(q, k - 1)
                gelu(HALF, 1)
                evacuate(HALF, 0)
                evacuate(HALF, 1)

            @block.vector
            def _(dve):
                dve.sem_inc(x_lo.sem, 2)
                dve.sem_inc(g_hi.sem, 4)
                dve.sem_inc(g_lo.sem, 4)
                step = [0]

                def link(ins):
                    step[0] += 1
                    ins.then_inc(table_dve, 1)
                    dve.wait_ge(table_dve, step[0])

                link(nc.vector.scalar_tensor_tensor(cnt, expert_id[:], -float(REGION), base[:], ALU.mult, ALU.add))
                link(nc.vector.tensor_scalar(cnt_i, cnt, float(BLK - 1), None, ALU.add))
                link(nc.vector.tensor_scalar(cnt_i, cnt_i, BLK.bit_length() - 1, None, ALU.arith_shift_right))
                link(nc.vector.tensor_copy(nblk, cnt_i))
                link(nc.vector.memset(rounded, 0.0))
                link(nc.vector.tensor_tensor_scan(cum, nblk, rounded, 0.0, ALU.add, ALU.add))
                link(nc.vector.tensor_scalar(jump, nblk, -float(BLK), float(REGION), ALU.mult, ALU.add))
                last_block = cum[0:1, E - 1:E]
                dve.wait_ge(iotas, 2)
                link(nc.vector.tensor_scalar(rounded[0:1, 0:1], last_block, -1.0, None, ALU.add))
                link(nc.vector.tensor_scalar(inner, number, rounded[0:1, 0:1], None, ALU.min))
                link(nc.vector.tensor_scalar(row, inner, float(BLK), None, ALU.mult))
                link(nc.vector.tensor_scalar(pick, inner, 0.0, None, ALU.mult))
                for e in range(E - 1):
                    link(nc.vector.tensor_scalar(extra, inner, cum[0:1, e:e + 1], jump[0:1, e:e + 1], ALU.is_ge, ALU.mult))
                    link(nc.vector.tensor_tensor(row, row, extra, ALU.add))
                    link(nc.vector.scalar_tensor_tensor(pick, inner, cum[0:1, e:e + 1], pick, ALU.is_ge, ALU.add))
                nc.vector.tensor_copy(from_row, row).then_inc(table_ok, 1)
                nc.vector.tensor_copy(which, pick).then_inc(table_ok, 1)
                nc.vector.tensor_copy(free_i, base[0:1]).then_inc(table_ok, 1)
                nc.vector.tensor_tensor(spread, logits[:], top[:, :, 0:1].to_broadcast([P, TILES, E]),
                                        ALU.subtract).then_inc(spread_ok, 1)
                nc.vector.tensor_tensor(ratio, top[:, :, 1], top[:, :, 0], ALU.subtract).then_inc(spread_ok, 1)

                def low(q, k):
                    dve.wait_ge(x_hi.sem, x_hi.at(2 * q + k))
                    dve.wait_ge(hid_ok.sem, hid_ok.at(2 * q + k - 2))
                    nc.vector.scalar_tensor_tensor(flat(xl[k % 2]), xt_bank[k % 2][:], S, flat(xh[k % 2]), ALU.mult,
                                                   ALU.subtract).then_inc(x_lo.sem, 1)

                def split(q, k):
                    for n in range(2):
                        dve.wait_ge(gelu_ok.sem, gelu_ok.at(2 * q + k, n + 1))
                        dve.wait_ge(y_ok.sem, y_ok.at(2 * q + k - 2))
                        nc.vector.tensor_scalar(flat(gh[k % 2][:, 2 * n:2 * n + 2]), flat(gel[k % 2][:, 2 * n:2 * n + 2]),
                                                S, None, ALU.mult).then_inc(g_hi.sem, 1)
                    for n in range(2):
                        dve.wait_ge(g_hi.sem, g_hi.at(2 * q + k, n + 1))
                        nc.vector.scalar_tensor_tensor(
                            flat(gl[k % 2][:, 2 * n:2 * n + 2]), flat(gel[k % 2][:, 2 * n:2 * n + 2]), S,
                            flat(gh[k % 2][:, 2 * n:2 * n + 2]), ALU.mult, ALU.subtract).then_inc(g_lo.sem, 1)

                low(0, 0)
                low(0, 1)
                split(0, 0)
                with dve.Fori(0, HALF) as q:
                    for k in (1, 2):
                        low(q, k + 1)
                        split(q, k)
                split(HALF, 1)
                link(nc.vector.tensor_copy(slot_y, flat(slots[:])))
                for e in range(E - 1):
                    link(nc.vector.tensor_scalar(past, flat(slots[:]), float((e + 1) * REGION), jump[:, e:e + 1],
                                                 ALU.is_ge, ALU.mult))
                    link(nc.vector.tensor_tensor(slot_y, slot_y, past, ALU.subtract))
                link(nc.vector.tensor_copy(flat(slots[:]), slot_y))
                dve.wait_ge(exp_ok, 2)
                link(nc.vector.tensor_reduce(denom, spread, AX.X, ALU.add))
                link(nc.vector.reciprocal(prob[:, 0], denom))
                link(nc.vector.tensor_tensor(prob[:, 1], prob[:, 0], ratio, ALU.mult))

            @block.tensor
            def _(pe):
                pe.sem_inc(rows_t.sem, 2)
                pe.sem_inc(hid_ok.sem, 4)
                pe.sem_inc(y_ok.sem, 2)
                pe.wait_ge(table_ok, 3)

                def turn(q, k):
                    s = k % 2
                    pe.wait_ge(rows_in[s].sem, rows_in[s].at(q + k // 2))
                    pe.wait_ge(x_lo.sem, x_lo.at(2 * q + k - 2))
                    for m in range(M):
                        for t in range(SUB):
                            last = nc.tensor.transpose(xt_bank[s][:, m * BLK + t * P:m * BLK + (t + 1) * P],
                                                       xin[s][:, t, m * P:(m + 1) * P], ident[:])
                    last.then_inc(rows_t.sem, 1)

                def up(q, k):
                    s = k % 2
                    e = pe.value_load(which[0:1, bass.ds(2 * q + k, 1)], min_val=0, max_val=E - 1)
                    pe.wait_ge(x_lo.sem, x_lo.at(2 * q + k))
                    for n in range(2):
                        pe.wait_ge(gelu_ok.sem, gelu_ok.at(2 * q + k - 2, n + 1))
                        for i in range(2):
                            f = 2 * n + i
                            dst = hid[s][n][:, i * BLK:(i + 1) * BLK]
                            for m in range(M):
                                cols = bass.ds(e * F + (m * E * F + f * P), P)
                                nc.tensor.matmul(dst, W1H[:, cols], xh[s][:, m], start=m == 0, stop=False)
                                nc.tensor.matmul(dst, W1H[:, cols], xl[s][:, m], start=False, stop=False)
                                last = nc.tensor.matmul(dst, W1L[:, cols], xh[s][:, m], start=False, stop=m == M - 1)
                        last.then_inc(hid_ok.sem, 1)

                def down(q, k):
                    s = k % 2
                    e = pe.value_load(which[0:1, bass.ds(2 * q + k, 1)], min_val=0, max_val=E - 1)
                    pe.wait_ge(g_lo.sem, g_lo.at(2 * q + k))
                    pe.wait_ge(y_sb.sem, y_sb.at(2 * q + k - 2))
                    for t in range(SUB):
                        dst = y_bank[s][:, t * C:(t + 1) * C]
                        tok = slice(t * P, (t + 1) * P)
                        for f in range(FC):
                            cols = bass.ds(e * C + f * E * C, C)
                            nc.tensor.matmul(dst, gh[s][:, f, tok], W2H[:, cols], start=f == 0, stop=False)
                            nc.tensor.matmul(dst, gh[s][:, f, tok], W2L[:, cols], start=False, stop=False)
                            last = nc.tensor.matmul(dst, gl[s][:, f, tok], W2H[:, cols], start=False, stop=f == FC - 1)
                    last.then_inc(y_ok.sem, 1)

                turn(0, 0)
                turn(0, 1)
                up(0, 0)
                with pe.Fori(0, HALF) as q:
                    for k in (1, 2):
                        turn(q, k + 1)
                        up(q, k)
                        down(q, k - 1)
                up(HALF, 1)
                down(HALF, 0)
                down(HALF, 1)

        at = [0]
        got = [place(at, [2 * J, C]) for _ in range(2)]
        mix = [place(at, [J, C]) for _ in range(2)]
        gain = [place(at, [C]) for _ in range(2)]
        index = [place(at, [2 * J], I32) for _ in range(2)]
        index_ok = count("index_ok", 1)
        gathered = [count(f"gathered{s}", 16 * 2 * J) for s in range(2)]
        gain_in = [count(f"gain_in{s}", 16) for s in range(2)]
        stored = [count(f"stored{s}", 16) for s in range(2)]
        first_ok, both_ok = count("first_ok", J), count("both_ok", J, 2)
        gained, summed = count("gained", 1), count("summed", 1, 2)

        with nc.Block() as block:

            @block.gpsimd
            def _(pool):
                def settle():
                    pool.sem_inc(pool_settled, 1)

                with pool.Fori(0, B // 2) as q:
                    for s in range(2):
                        b = 2 * q + s
                        pool.wait_ge(both_ok.sem, both_ok.at(b - 2))
                        settle()
                        nc.gpsimd.tensor_copy(index[s], flat(slots[:, bass.ds(b, 1), :])).then_inc(index_ok.sem, 1)
                        pool.wait_ge(index_ok.sem, index_ok.at(b))
                        settle()
                        for n in range(2 * J):
                            pool.indirect_dma_start(got[s][:, n], None, sorted_y, bass.IndirectOffsetOnAxis(
                                ap=index[s][:, n:n + 1], axis=0)).then_inc(gathered[s].sem, 16)

            @block.scalar
            def _(act):
                with act.Fori(0, B // 2) as q:
                    for s in range(2):
                        b = 2 * q + s
                        act.wait_ge(gathered[s].sem, gathered[s].at(q))
                        if s is not None:
                            act.wait_ge(summed.sem, summed.at(b - 2))
                        for j in range(J):
                            nc.scalar.activation(mix[s][:, j], got[s][:, j], ACT.Copy,
                                                 scale=prob[:, 0, bass.ds(b * J + j, 1)]).then_inc(first_ok.sem, 1)

            @block.vector
            def _(dve):
                dve.sem_inc(both_ok.sem, 2 * J)
                dve.sem_inc(summed.sem, 2)
                with dve.Fori(0, B // 2) as q:
                    for s in range(2):
                        b = 2 * q + s
                        dve.wait_ge(gathered[s].sem, gathered[s].at(q))
                        for j in range(J):
                            dve.wait_ge(first_ok.sem, first_ok.at(b, j + 1))
                            nc.vector.scalar_tensor_tensor(mix[s][:, j], got[s][:, J + j],
                                                           prob[:, 1, bass.ds(b * J + j, 1)], mix[s][:, j], ALU.mult,
                                                           ALU.add).then_inc(both_ok.sem, 1)
                        dve.wait_ge(both_ok.sem, both_ok.at(b))
                        dve.wait_ge(gain_in[s].sem, gain_in[s].at(q))
                        nc.vector.tensor_tensor(mix[s], mix[s], gain[s].unsqueeze(1).to_broadcast([P, J, C]),
                                                ALU.mult).then_inc(gained.sem, 1)
                        dve.wait_ge(gained.sem, gained.at(b))
                        xb = X[:, bass.ds(b * J, J), :]
                        nc.vector.tensor_tensor(xb, xb, mix[s], ALU.add).then_inc(summed.sem, 1)

            @block.sync
            def _(sp):
                with sp.Fori(0, B // 2) as q:
                    for s in range(2):
                        b = 2 * q + s
                        sp.wait_ge(summed.sem, summed.at(b - 2))
                        sp.dma_start(gain[s], mod_rows[bass.ds(b, 1), 3 * C:4 * C].to_broadcast([P, C])
                                     ).then_inc(gain_in[s].sem, 16)
                    for s in range(2):
                        b = 2 * q + s
                        sp.wait_ge(summed.sem, summed.at(b))
                        sp.dma_start(out[bass.ds(b * T, T), :].rearrange("(j p) c -> p j c", p=P),
                                     X[:, bass.ds(b * J, J), :]).then_inc(stored[s].sem, 16)
                for s in range(2):
                    sp.wait_ge(stored[s].sem, 16 * B // 2)


_IN = {
    "x": "L0_attn_x", "wi": "L0_attn_Wi", "wf": "L0_attn_Wf", "wg": "L0_attn_Wg", "conv_i": "L0_attn_conv_i",
    "conv_f": "L0_attn_conv_f", "gnorm": "L0_attn_g_norm_weight", "wo": "L0_attn_Wo", "gamma": "L0_ffn_ln_gamma",
    "beta": "L0_ffn_ln_beta", "gate": "L0_ffn_gate_w", "w1": "L0_ffn_w1", "w2": "L0_ffn_w2", "c_t": "L0_c",
    "wmod": "L0_wmod",
}


def lay_out(inputs):
    a = {k: np.asarray(inputs[v]) for k, v in _IN.items()}
    a["x"] = a["x"].reshape(N, C)
    for name in ("gnorm", "gamma", "beta"):
        a[name] = a[name].reshape(M, P).T
    a["gate"] = a["gate"].T
    a["c_t"] = a["c_t"].T
    a["w1"] = a["w1"].transpose(2, 0, 1).reshape(C, E * F)
    a["w2"] = a["w2"].transpose(2, 0, 1).reshape(F, E * C)
    return {k: np.ascontiguousarray(v) for k, v in a.items()}


def kernel(**inputs):
    import concourse.bacc as bacc
    from concourse.bass_utils import run_bass_kernel_spmd

    nc = bacc.Bacc("TRN2", target_bir_lowering=False, num_devices=1)
    arrays = lay_out(inputs)
    aps = {k: nc.dram_tensor(f"in_{k}", a.shape, mybir.dt.from_np(a.dtype), kind="ExternalInput").ap()
           for k, a in arrays.items()}
    out = nc.dram_tensor("out_x", (N, C), F32, kind="ExternalOutput").ap()
    build(nc, out=out, **aps)
    got = run_bass_kernel_spmd(nc, [{f"in_{k}": a for k, a in arrays.items()}], core_ids=[0])
    return got.results[0]["out_x"].reshape(B, T, C)
```

```python
from contextlib import ExitStack

import numpy as np

import concourse.bass as bass
from concourse import mybir

F32, F16, I32, U32 = mybir.dt.float32, mybir.dt.float16, mybir.dt.int32, mybir.dt.uint32
ALU = mybir.AluOpType
ACT = mybir.ActivationFunctionType
AX = mybir.AxisListType

P = 128
B, T, C = 16, 512, 256
E, F = 8, 512
TAPS = 4
EPS = 1e-5
M = C // P
J = T // P
TILES = B * J
N = B * T
FC = F // P
BLK = 256
SUB = BLK // P
REGION = N + BLK
BLOCKS = 2 * N // BLK + E - 1
LOOP_BLOCKS = BLOCKS + BLOCKS % 2
ZW = TAPS - 1 + T
STAGE = (M * E * F + FC * E * C) // B
HW = ZW + 1
ARENA = 15056
S = 64.0
S2 = S * S


class Count:

    def __init__(self, sem, per, lead=0):
        self.sem, self.per, self.lead = sem, per, lead

    def at(self, rnd, n=None):
        n = self.per if n is None else n
        return rnd * self.per + (self.lead * self.per + n)

    def wait(self, eng, rnd, n=None):
        if not (isinstance(rnd, int) and rnd + self.lead < 0):
            eng.wait_ge(self.sem, self.at(rnd, n))


def build(nc, x, wi, wf, wg, conv_i, conv_f, conv_f_rows, gnorm, wo, gamma, beta, gate, w12, c_t, wmod, out):
    with ExitStack() as ctx:
        def sb(name, shape, dt=F32):
            return ctx.enter_context(nc.sbuf_tensor(name, shape, dt))

        def ps(name):
            return ctx.enter_context(nc.psum_tensor(name, [P, 512], F32))

        def sem(name):
            return ctx.enter_context(nc.semaphore(name))

        def count(name, per, lead=0):
            return Count(sem(name), per, lead)

        mod_rows = nc.dram_tensor("mod_rows", [B, 4 * C], F32, kind="Internal").ap()
        sorted_x = nc.dram_tensor("sorted_x", [E * REGION, C], F32, kind="Internal").ap()
        sorted_y = nc.dram_tensor("sorted_y", [LOOP_BLOCKS * BLK, C], F32, kind="Internal").ap()

        X = sb("X", [P, TILES, C])
        WEH = sb("WEH", [P, B * STAGE], F16)
        WEL = sb("WEL", [P, B * STAGE], F16)
        W2_AT = M * E * F
        WPH = sb("WPH", [P, 2, M, C], F16)
        WPL = sb("WPL", [P, 2, M, C], F16)
        WFH = sb("WFH", [P, TAPS, M, C], F16)
        WFL = sb("WFL", [P, TAPS, M, C], F16)
        WOH = sb("WOH", [P, M, C], F16)
        WOL = sb("WOL", [P, M, C], F16)
        ident = sb("ident", [P, P])
        ones = sb("ones", [P, P])
        before = sb("before", [P, P], F16)
        ones16 = sb("ones16", [P, P], F16)
        expert_id = sb("expert_id", [P, E])
        minus_half = sb("minus_half", [P, J])
        conv = sb("conv", [P, M, TAPS])
        h_scale = sb("h_scale", [P, M, B])
        bias = sb("bias", [P, 4, M, B])
        pad_h = sb("pad_h", [P, M, B], F16)
        pad_l = sb("pad_l", [P, M, B], F16)
        gate_c = sb("gate_c", [P, M, E + 1])
        gate_b = sb("gate_b", [P, E])
        logits = sb("logits", [P, TILES, E])
        top = sb("top", [P, TILES, 2])
        slots = sb("slots", [P, B, 2 * J], I32)
        scale_y = sb("scale_y", [P, M])
        prob = sb("prob", [P, 2, TILES])
        base = sb("base", [P, E])

        arena = sb("arena", [P, ARENA])

        def place(cursor, shape, dt=F32):
            n = int(np.prod(shape))
            words = n if dt != F16 else n // 2
            ap = arena[:, cursor[0]:cursor[0] + words]
            cursor[0] += words
            assert cursor[0] <= ARENA
            if dt != F32:
                ap = ap.bitcast(dt)
            if len(shape) == 2:
                ap = ap.rearrange("p (a b) -> p a b", b=shape[1])
            if len(shape) == 3:
                ap = ap.rearrange("p (a b c) -> p a b c", b=shape[1], c=shape[2])
            return ap

        bank = [ps(f"bank{n}") for n in range(8)]

        def flat(ap):
            return ap.rearrange("p a b -> p (a b)")

        at = [0]
        c_in = place(at, [M, B])
        silu_c = place(at, [M, B])
        shift_t = place(at, [M, B])
        w_mod = place(at, [M, 6 * C])
        w_in = place(at, [4, M * C])
        taps_f = place(at, [TAPS, C])
        w_tap = place(at, [TAPS, M * C])
        conv_fc = place(at, [M, TAPS])
        tap_sum = place(at, [M])
        norm_w = place(at, [M])
        gamma_c = place(at, [M])
        beta_c = place(at, [M])
        gate_t = place(at, [M, E])
        gate_gb = place(at, [M, 2 * E])
        rows_sb = place(at, [4, C])[0:B]
        sign_sb = place(at, [2, C])[0:B]

        consts = sem("consts")
        small_in = sem("small_in")
        c_ok, mod_ok, mod_sb, bias_ok, bias_sb = map(sem, ("c_ok", "mod_ok", "mod_sb", "bias_ok", "bias_sb"))
        gate_ok, gate_in = sem("gate_ok"), sem("gate_in")
        rows_ok, rows_out = sem("rows_ok"), sem("rows_out")
        wo_ok, tap_ok, split_hi = sem("wo_ok"), sem("tap_ok"), sem("split_hi")
        pad_ok = sem("pad_ok")
        setup_dve = sem("setup_dve")
        SMALL = 14
        x_in = count("x_in", 16)

        with nc.Block() as block:

            @block.sync
            def _(sp):
                loads = [
                    (c_in, c_t.rearrange("(k p) b -> p k b", p=P)),
                    (w_mod, wmod.rearrange("(k p) n -> p k n", p=P)),
                ] + [(w_in[:, n].rearrange("p (k n) -> p k n", k=M), w.rearrange("(k p) n -> p k n", p=P))
                     for n, w in enumerate((wi, wg, wf, wo))] + [
                    (conv_fc, conv_f.rearrange("(m p) k -> p m k", p=P)),
                    (conv[:], conv_i.rearrange("(m p) k -> p m k", p=P)),
                    (taps_f.rearrange("p k c -> p (k c)"), conv_f_rows.to_broadcast([P, TAPS * C])),
                    (norm_w, gnorm),
                    (gamma_c, gamma),
                    (beta_c, beta),
                    (gate_t, gate.rearrange("(m p) e -> p m e", p=P)),
                ]
                assert len(loads) == SMALL - 1
                for n, (dst, src) in enumerate(loads):
                    sp.dma_start(dst, src).then_inc(small_in, 16)
                sp.dma_start(X[:, 0:J, :], x[0:T, :].rearrange("(j p) c -> p j c", p=P)).then_inc(x_in.sem, 16)
                sp.wait_ge(rows_ok, 1)
                sp.dma_start(mod_rows.rearrange("b (q c) -> b q c", q=4), rows_sb).then_inc(rows_out, 16)
                sp.wait_ge(rows_out, 16)

            @block.gpsimd
            def _(pool):
                nc.gpsimd.memset(ident[:], 0.0).then_inc(consts, 1)
                nc.gpsimd.memset(ones[:], 1.0).then_inc(consts, 1)
                nc.gpsimd.memset(ones16[:], 1.0).then_inc(consts, 1)
                nc.gpsimd.memset(minus_half[:], -0.5).then_inc(consts, 1)
                nc.gpsimd.iota(expert_id[:], pattern=[[1, E]], base=0, channel_multiplier=0,
                               allow_small_or_imprecise_dtypes=True).then_inc(consts, 1)
                nc.gpsimd.iota(base[:], pattern=[[REGION, E]], base=0, channel_multiplier=0,
                               allow_small_or_imprecise_dtypes=True).then_inc(consts, 1)
                pool.wait_ge(consts, 6)
                nc.gpsimd.affine_select(out=ident[:], in_=ident[:], compare_op=ALU.not_equal, fill=1.0,
                                        base=0, pattern=[[-1, P]], channel_multiplier=1).then_inc(consts, 1)
                nc.gpsimd.affine_select(out=before[:], in_=ones16[:], compare_op=ALU.is_gt, fill=0.0,
                                        base=0, pattern=[[1, P]], channel_multiplier=-1).then_inc(consts, 1)
                pool.wait_ge(consts, 8)

            @block.scalar
            def _(act):
                nc.scalar.preload_act_table(ACT.Silu)
                act.wait_ge(small_in, 16 * (SMALL - 1))
                nc.scalar.activation(silu_c, c_in, ACT.Silu).then_inc(c_ok, 1)
                for n in range(2):
                    nc.scalar.activation(flat(WPH[:, n]), w_in[:, n], ACT.Copy, scale=S).then_inc(split_hi, 1)
                act.wait_ge(wo_ok, M)
                nc.scalar.activation(flat(WOH[:]), w_in[:, 3], ACT.Copy).then_inc(split_hi, 1)
                for k in range(TAPS):
                    act.wait_ge(tap_ok, M * (k + 1))
                    nc.scalar.activation(flat(WFH[:, k]), w_tap[:, k], ACT.Copy, scale=S).then_inc(split_hi, 1)
                act.wait_ge(mod_sb, 2)
                nc.scalar.activation(flat(pad_h[:]), flat(shift_t), ACT.Copy, scale=-S).then_inc(pad_ok, 1)

            @block.tensor
            def _(pe):
                pe.wait_ge(c_ok, 1)
                for q in range(2 * M):
                    for k in range(M):
                        nc.tensor.matmul(bank[2][:, q * B:(q + 1) * B], w_mod[:, k, q * P:(q + 1) * P],
                                         silu_c[:, k], start=k == 0, stop=k == M - 1).then_inc(mod_ok, 1)
                for q in range(2):
                    for k in range(M):
                        nc.tensor.matmul(bank[q][0:B, :], silu_c[:, k],
                                         w_mod[:, k, (1 + q) * 2 * C:(2 + q) * 2 * C], start=k == 0,
                                         stop=k == M - 1).then_inc(mod_ok, 1)
                pe.wait_ge(mod_sb, 2)
                for n in range(3 * M):
                    p, m = divmod(n, M)
                    for k in range(M):
                        nc.tensor.matmul(bank[3][:, n * B:(n + 1) * B], w_in[:, p, k * C + m * P:k * C + (m + 1) * P],
                                         shift_t[:, k], start=k == 0, stop=k == M - 1).then_inc(bias_ok, 1)
                pe.wait_ge(gate_in, 2 * M)
                pe.wait_ge(consts, 8)
                for k in range(M):
                    nc.tensor.matmul(bank[4][:, 0:2 * E], ones[:], gate_gb[:, k], start=k == 0,
                                     stop=k == M - 1).then_inc(gate_ok, 1)

            @block.vector
            def _(dve):
                step = [0]

                def link(ins):
                    step[0] += 1
                    ins.then_inc(setup_dve, 1)
                    dve.wait_ge(setup_dve, step[0])

                dve.wait_ge(small_in, 16 * (SMALL - 1))
                for k in range(M):
                    nc.vector.tensor_scalar(gate_gb[:, k, 0:E], gate_t[:, k], gamma_c[:, k:k + 1], None,
                                            ALU.mult).then_inc(gate_in, 1)
                    nc.vector.tensor_scalar(gate_gb[:, k, E:2 * E], gate_t[:, k], beta_c[:, k:k + 1], None,
                                            ALU.mult).then_inc(gate_in, 1)
                for k in range(M):
                    nc.vector.tensor_scalar(w_in[:, 3, k * C:(k + 1) * C], w_in[:, 3, k * C:(k + 1) * C],
                                            norm_w[:, k:k + 1], -0.5 * S, ALU.mult, ALU.mult).then_inc(wo_ok, 1)
                for k in range(TAPS):
                    for m in range(M):
                        cols = slice(m * C, (m + 1) * C)
                        nc.vector.tensor_tensor(w_tap[:, k, cols], w_in[:, 2, cols], taps_f[:, k],
                                                ALU.mult).then_inc(tap_ok, 1)
                link(nc.vector.tensor_reduce(tap_sum, conv_fc, AX.X, ALU.add))
                dve.wait_ge(mod_ok, 2 * M * M)
                nc.vector.tensor_copy(flat(shift_t), bank[2][:, 0:M * B]).then_inc(mod_sb, 1)
                nc.vector.tensor_scalar(flat(h_scale[:]), bank[2][:, M * B:2 * M * B], 1.0, S, ALU.add,
                                        ALU.mult).then_inc(mod_sb, 1)
                dve.wait_ge(mod_ok, 2 * M + 2 * M * M)
                for q, r, z in ((0, 0, 0), (1, 3, C)):
                    gain = bank[q][0:B, z:z + C]
                    link(nc.vector.tensor_scalar(sign_sb[:, 0], gain, 0.0, 2.0, ALU.is_ge, ALU.mult))
                    link(nc.vector.tensor_scalar(sign_sb[:, 1], gain, -1.0, 0.25, ALU.mult, ALU.max))
                    link(nc.vector.tensor_tensor(sign_sb[:, 1], sign_sb[:, 1], gain, ALU.max))
                    link(nc.vector.scalar_tensor_tensor(rows_sb[:, r], sign_sb[:, 0], -1.0, sign_sb[:, 1],
                                                        ALU.add, ALU.mult))
                link(nc.vector.tensor_copy(rows_sb[:, 1], bank[0][0:B, C:2 * C]))
                nc.vector.tensor_scalar(rows_sb[:, 2], bank[1][0:B, 0:C], 1.0, None, ALU.add).then_inc(rows_ok, 1)
                dve.wait_ge(pad_ok, 1)
                nc.vector.scalar_tensor_tensor(flat(pad_l[:]), flat(shift_t), -S, flat(pad_h[:]), ALU.mult,
                                               ALU.subtract).then_inc(bias_sb, 1)
                dve.wait_ge(bias_ok, 3 * M * M)
                sums = bank[3][:, 0:3 * M * B].rearrange("p (n m b) -> p n m b", n=3, m=M)
                link(nc.vector.tensor_copy(bias[:, 0:2].rearrange("p n m b -> p (n m b)"), bank[3][:, 0:2 * M * B]))
                for m in range(M):
                    nc.vector.tensor_scalar(bias[:, 2, m], sums[:, 2, m], tap_sum[:, m:m + 1], 0.5, ALU.mult,
                                            ALU.mult).then_inc(bias_sb, 1)
                    nc.vector.tensor_scalar(bias[:, 3, m], sums[:, 0, m], conv[:, m, TAPS - 1:TAPS], None,
                                            ALU.mult).then_inc(bias_sb, 1)
                nc.vector.tensor_scalar(scale_y[:], conv[:, :, TAPS - 1], 1 / S2, None, ALU.mult).then_inc(bias_sb, 1)
                dve.wait_ge(gate_ok, M)
                dve.wait_ge(gate_in, 2 * M)
                nc.vector.tensor_copy(gate_b[:], bank[4][:, E:2 * E]).then_inc(bias_sb, 1)
                nc.vector.memset(gate_c[:, :, E:E + 1], 1.0).then_inc(bias_sb, 1)
                for k in range(M):
                    nc.vector.scalar_tensor_tensor(gate_c[:, k, 0:E], bank[4][:, 0:E], -1.0 / C, gate_gb[:, k, 0:E],
                                                   ALU.mult, ALU.add).then_inc(bias_sb, 1)
                dve.wait_ge(split_hi, 2)
                for n in range(2):
                    nc.vector.scalar_tensor_tensor(flat(WPL[:, n]), w_in[:, n], S, flat(WPH[:, n]), ALU.mult,
                                                   ALU.subtract).then_inc(bias_sb, 1)
                dve.wait_ge(split_hi, 3)
                dve.wait_ge(wo_ok, M)
                nc.vector.tensor_tensor(flat(WOL[:]), w_in[:, 3], flat(WOH[:]), ALU.subtract).then_inc(bias_sb, 1)
                dve.wait_ge(tap_ok, M * TAPS)
                for k in range(TAPS):
                    dve.wait_ge(split_hi, 4 + k)
                    nc.vector.scalar_tensor_tensor(flat(WFL[:, k]), w_tap[:, k], S, flat(WFH[:, k]), ALU.mult,
                                                   ALU.subtract).then_inc(bias_sb, 1)

        at = [0]
        xn = place(at, [J, C])
        hh, hl = place(at, [M, HW], F16), place(at, [M, HW], F16)
        z = place(at, [M, ZW])
        y = place(at, [M, T])
        sg = place(at, [M, T])
        th = place(at, [M, T])
        sq = place(at, [M, T])
        attn = place(at, [J, C])
        uh, ul = place(at, [M, T], F16), place(at, [M, T], F16)
        mod_ga = place(at, [C])
        mod_cs = place(at, [2, C])
        h2 = place(at, [J, C])
        h2_tsb = place(at, [M, T])
        h2_sq = place(at, [M, T])
        w_stage = place(at, [STAGE])
        bns1, bns2 = place(at, [J, 6]), place(at, [J, 6])
        mv1, mv2 = place(at, [J, 2]), place(at, [J, 2])
        r1, r2, r3, rms = (place(at, [J]) for _ in range(4))
        v1, v2, v3, v4, mean3 = (place(at, [J]) for _ in range(5))
        off1, off2 = place(at, [J]), place(at, [J])
        picks = place(at, [J, 8], U32)
        picks_f = place(at, [2, J])
        hot = place(at, [2 * J, E])
        ranked_hot = place(at, [2 * J, E])
        hot2 = place(at, [J, E], F16)
        rank = place(at, [J, E])
        logit_b, top_b = place(at, [J, E]), place(at, [J, E])
        slots_f = place(at, [2 * J])
        slots_b = place(at, [2 * J], I32)
        tp, prj, opj = bank[0:2], bank[2:4], bank[4:6]
        ssq = bank[6][:, 0:J]
        W9 = E + 1
        score = bank[7][:, 0:J * W9].rearrange("p (j e) -> p j e", e=W9)
        square = bank[7][:, J * W9:J * W9 + J]
        ahead = bank[7][:, 64:64 + J * E]
        total = bank[7][:, 128:128 + E]

        pads = sem("pads")
        dve_settled, pool_settled = sem("dve_settled"), sem("pool_settled")
        ga_in, cs_in, stage_in = count("ga_in", 16), count("cs_in", 16), count("stage_in", 16)
        stage_hi, stage_scaled, stage_lo = count("stage_hi", 1), count("stage_scaled", 1), count("stage_lo", 1)
        stats1, moments1 = count("stats1", J), count("moments1", J)
        var1, rstd1, off1_ok = count("var1", 1), count("rstd1", 1), count("off1_ok", 1)
        normed = count("normed", J)
        xn_t = count("xn_t", M)
        h_hi, h_lo = count("h_hi", M + 1), count("h_lo", M + 1)
        projected = count("projected", 6)
        evac = count("evac", 8)
        conv_ok = count("conv_ok", M * (TAPS - 1))
        silu_i, forget_ok, gate_i = count("silu_i", M), count("forget_ok", M), count("gate_i", M)
        scanned = count("scanned", M)
        sq_ok, ssq_ok = count("sq_ok", M), count("ssq_ok", 1)
        rms_in, rms_ok = count("rms_in", 1), count("rms_ok", 1)
        u_ok, u_hi, u_lo = count("u_ok", M), count("u_hi", M), count("u_lo", M)
        o_ok = count("o_ok", 2)
        attn_ok = count("attn_ok", J)
        x1_ok = count("x1_ok", 1)
        stats2, moments2 = count("stats2", J), count("moments2", J)
        var2, rstd2, off2_ok = count("var2", 1), count("rstd2", 1), count("off2_ok", 1)
        normed2, scaled2, h2_ok = count("normed2", J), count("scaled2", 1), count("h2_ok", 1)
        h2_t, h2_sb = count("h2_t", M), count("h2_sb", 2 * M)
        scored, mean_ok, var3, rstd3 = count("scored", 1), count("mean_ok", 1), count("var3", 2), count("rstd3", 1)
        mean_sq = count("mean_sq", 1)
        score_in, top_ok, picked = count("score_in", J), count("top_ok", J), count("picked", J)
        kept, pick_f = count("kept", 2), count("pick_f", 2)
        hot_ok, hot2_ok = count("hot_ok", 2), count("hot2_ok", 1)
        counted, rank_ok, base_ok = count("counted", 1), count("rank_ok", 1), count("base_ok", 1)
        own_rank, slot_f, slot_ok = count("own_rank", 2), count("slot_f", 1), count("slot_ok", 2)
        scattered = count("scattered", 16 * 2 * J)

        def steps(eng, step, ahead=1):
            step(-1)
            step(0)
            step(1)
            with eng.Fori(2, B - ahead) as t:
                step(t)
            for t in range(B - ahead, B + 1):
                step(t)

        def has(b):
            return not isinstance(b, int) or 0 <= b < B

        with nc.Block() as block:

            @block.sync
            def _(sp):
                def step(t):
                    a, b, c = t + 1, t, t - 1
                    if has(t + 2):
                        x_in.wait(sp, t + 1)
                        sp.dma_start(X[:, bass.ds((t + 2) * J, J), :],
                                     x[bass.ds((t + 2) * T, T), :].rearrange("(j p) c -> p j c", p=P)
                                     ).then_inc(x_in.sem, 16)
                    if has(b):
                        h2_ok.wait(sp, c)
                        cs_in.wait(sp, c)
                        sp.dma_start(mod_cs.rearrange("p q c -> p (q c)"),
                                     mod_rows[bass.ds(b, 1), C:3 * C].to_broadcast([P, 2 * C])
                                     ).then_inc(cs_in.sem, 16)
                    if has(a):
                        stage_lo.wait(sp, b)
                        stage_in.wait(sp, b)
                        sp.dma_start(w_stage, w12[bass.ds(a * P, P), :]).then_inc(stage_in.sem, 16)
                        attn_ok.wait(sp, b)
                        ga_in.wait(sp, b)
                        sp.dma_start(mod_ga, mod_rows[bass.ds(a, 1), 0:C].to_broadcast([P, C])
                                     ).then_inc(ga_in.sem, 16)

                steps(sp, step, ahead=2)

            @block.gpsimd
            def _(pool):
                def settle():
                    pool.sem_inc(pool_settled, 1)

                def rstd(b, moments, mv, v, var, r, ok):
                    moments.wait(pool, b)
                    settle()
                    nc.gpsimd.tensor_scalar(v, mv[:, :, 1], EPS, None, ALU.add).then_inc(var.sem, 1)
                    var.wait(pool, b)
                    nc.gpsimd.tensor_tensor(r, v, minus_half[:], ALU.pow).then_inc(ok.sem, 1)

                def step(t):
                    a, b, c = t + 1, t, t - 1
                    if has(a):
                        rstd(a, moments1, mv1, v1, var1, r1, rstd1)
                    if has(c):
                        rstd(c, moments2, mv2, v2, var2, r2, rstd2)
                        scaled2.wait(pool, c)
                        cs_in.wait(pool, c)
                        nc.gpsimd.tensor_tensor(h2, h2, mod_cs[:, 0:1].to_broadcast([P, J, C]),
                                                ALU.add).then_inc(h2_ok.sem, 1)
                    if has(b):
                        rms_in.wait(pool, b)
                        nc.gpsimd.tensor_tensor(rms, v4, minus_half[:], ALU.pow).then_inc(rms_ok.sem, 1)
                        stage_hi.wait(pool, b)
                        settle()
                        nc.gpsimd.tensor_scalar(w_stage, w_stage, S, None, ALU.mult).then_inc(stage_scaled.sem, 1)
                    if has(c):
                        var3.wait(pool, c)
                        nc.gpsimd.tensor_tensor(r3, v3, minus_half[:], ALU.pow).then_inc(rstd3.sem, 1)
                    if has(b):
                        stage_scaled.wait(pool, b)
                        settle()
                        cols = bass.ds(b * STAGE, STAGE)
                        nc.gpsimd.tensor_tensor(WEL[:, cols], w_stage, WEH[:, cols],
                                                ALU.subtract).then_inc(stage_lo.sem, 1)
                        attn_ok.wait(pool, b)
                        settle()
                        xb = X[:, bass.ds(b * J, J), :]
                        nc.gpsimd.tensor_tensor(xb, xb, attn, ALU.add).then_inc(x1_ok.sem, 1)
                    if has(c):
                        slot_ok.wait(pool, c, 1)
                        settle()
                        for n in range(2 * J):
                            pool.indirect_dma_start(sorted_x, bass.IndirectOffsetOnAxis(ap=slots_b[:, n:n + 1], axis=0),
                                                    h2[:, n % J], None).then_inc(scattered.sem, 16)

                steps(pool, step)

            @block.scalar
            def _(act):
                nc.scalar.preload_act_table(ACT.Silu)

                def step(t):
                    a, b, c = t + 1, t, t - 1
                    if has(b):
                        stage_in.wait(act, b)
                        nc.scalar.activation(WEH[:, bass.ds(b * STAGE, STAGE)], w_stage, ACT.Copy,
                                             scale=S).then_inc(stage_hi.sem, 1)
                        for m in range(M):
                            conv_ok.wait(act, b, M * (TAPS - 2) + m + 1)
                            nc.scalar.activation(y[:, m], y[:, m], ACT.Silu).then_inc(silu_i.sem, 1)
                    if has(a):
                        off1_ok.wait(act, a)
                        rstd1.wait(act, a)
                        xn_t.wait(act, a - 1)
                        for j in range(J):
                            nc.scalar.activation(xn[:, j], flat(X[:, bass.ds(a * J + j, 1), :]), ACT.Identity,
                                                 scale=r1[:, j:j + 1], bias=off1[:, j:j + 1]).then_inc(normed.sem, 1)
                    if has(c):
                        off2_ok.wait(act, c)
                        rstd2.wait(act, c)
                        scattered.wait(act, c - 1)
                        h2_t.wait(act, c - 1)
                        for j in range(J):
                            nc.scalar.activation(h2[:, j], flat(X[:, bass.ds(c * J + j, 1), :]), ACT.Identity,
                                                 scale=r2[:, j:j + 1], bias=off2[:, j:j + 1]).then_inc(normed2.sem, 1)
                    if has(a):
                        projected.wait(act, a - 1)
                        nc.scalar.activation(hh[:, :, 0:HW - T], pad_h[:, :, bass.ds(a, 1)].to_broadcast([P, M, HW - T]),
                                             ACT.Copy).then_inc(h_hi.sem, 1)
                        for m in range(M):
                            xn_t.wait(act, a, m + 1)
                            nc.scalar.activation(hh[:, m, HW - T:HW], tp[m][:], ACT.Copy,
                                                 scale=h_scale[:, m, bass.ds(a, 1)]).then_inc(h_hi.sem, 1)
                    if has(b):
                        for m in range(M):
                            scanned.wait(act, b, m + 1)
                            ssq_ok.wait(act, b - 1)
                            nc.scalar.activation(sq[:, m], y[:, m], ACT.Square).then_inc(sq_ok.sem, 1)
                        for m in range(M):
                            u_ok.wait(act, b, m + 1)
                            o_ok.wait(act, b - 1)
                            nc.scalar.activation(uh[:, m], sg[:, m], ACT.Copy, scale=S).then_inc(u_hi.sem, 1)
                    if has(c):
                        for m in range(M):
                            h2_t.wait(act, c, m + 1)
                            scored.wait(act, c - 1)
                            nc.scalar.activation(h2_tsb[:, m], tp[m][:], ACT.Copy).then_inc(h2_sb.sem, 1)
                            nc.scalar.activation(h2_sq[:, m], tp[m][:], ACT.Square).then_inc(h2_sb.sem, 1)
                    if has(a):
                        for m in range(M):
                            projected.wait(act, a, m + 1)
                            conv_ok.wait(act, a - 1)
                            nc.scalar.activation(z[:, m, ZW - T:ZW], prj[m][:], ACT.Identity, scale=1 / S2,
                                                 bias=bias[:, 0, m, bass.ds(a, 1)]).then_inc(evac.sem, 1)
                            u_ok.wait(act, a - 1)
                            sq_ok.wait(act, a - 1)
                            nc.scalar.activation(y[:, m], prj[m][:], ACT.Identity, scale=scale_y[:, m:m + 1],
                                                 bias=bias[:, 3, m, bass.ds(a, 1)]).then_inc(evac.sem, 1)
                        for m in range(M):
                            projected.wait(act, a, M + m + 1)
                            u_lo.wait(act, a - 1)
                            nc.scalar.activation(sg[:, m], prj[m][:], ACT.Silu, scale=1 / S2,
                                                 bias=bias[:, 1, m, bass.ds(a, 1)]).then_inc(evac.sem, 1)
                        for m in range(M):
                            projected.wait(act, a, 2 * M + m + 1)
                            scanned.wait(act, a - 1)
                            nc.scalar.activation(th[:, m], prj[m][:], ACT.Tanh, scale=0.5 / S2,
                                                 bias=bias[:, 2, m, bass.ds(a, 1)]).then_inc(evac.sem, 1)

                steps(act, step)

            @block.vector
            def _(dve):
                nc.vector.memset(z[:, :, 0:ZW - T], 0.0).then_inc(pads, 1)
                dve.wait_ge(pads, 1)

                def settle():
                    dve.sem_inc(dve_settled, 1)

                def step(t):
                    a, b, c = t + 1, t, t - 1
                    if has(b):
                        for k in range(1, TAPS):
                            for m in range(M):
                                if k == 1:
                                    evac.wait(dve, b, 2 * m + 2)
                                else:
                                    conv_ok.wait(dve, b, (k - 2) * M + m + 1)
                                nc.vector.scalar_tensor_tensor(
                                    y[:, m], z[:, m, ZW - T - k:ZW - k], conv[:, m, TAPS - 1 - k:TAPS - k],
                                    y[:, m], ALU.mult, ALU.add).then_inc(conv_ok.sem, 1)
                    if has(a):
                        x_in.wait(dve, a)
                        settle()
                        for j in range(J):
                            nc.vector.bn_stats(bns1[:, j], flat(X[:, bass.ds(a * J + j, 1), :])).then_inc(stats1.sem, 1)
                    if has(b):
                        for m in range(M):
                            silu_i.wait(dve, b, m + 1)
                            evac.wait(dve, b, 3 * M + m + 1)
                            nc.vector.scalar_tensor_tensor(y[:, m], th[:, m], -1.0, y[:, m], ALU.add,
                                                           ALU.mult).then_inc(gate_i.sem, 1)
                    if has(a):
                        for j in range(J):
                            stats1.wait(dve, a, j + 1)
                            settle()
                            nc.vector.bn_aggr(mv1[:, j], bns1[:, j]).then_inc(moments1.sem, 1)
                    if has(b):
                        for m in range(M):
                            gate_i.wait(dve, b, m + 1)
                            nc.vector.tensor_scalar(th[:, m], th[:, m], 0.5, 0.5, ALU.mult,
                                                    ALU.add).then_inc(forget_ok.sem, 1)
                    if has(c):
                        x1_ok.wait(dve, c)
                        settle()
                        for j in range(J):
                            nc.vector.bn_stats(bns2[:, j], flat(X[:, bass.ds(c * J + j, 1), :])).then_inc(stats2.sem, 1)
                        for j in range(J):
                            stats2.wait(dve, c, j + 1)
                            settle()
                            nc.vector.bn_aggr(mv2[:, j], bns2[:, j]).then_inc(moments2.sem, 1)
                    if has(b):
                        for m in range(M):
                            forget_ok.wait(dve, b, m + 1)
                            nc.vector.tensor_tensor_scan(y[:, m], th[:, m], y[:, m], 0.0, ALU.mult,
                                                         ALU.add).then_inc(scanned.sem, 1)
                    if has(a):
                        rstd1.wait(dve, a)
                        moments1.wait(dve, a)
                        nc.vector.scalar_tensor_tensor(off1, mv1[:, :, 0], -1.0, r1, ALU.mult,
                                                       ALU.mult).then_inc(off1_ok.sem, 1)
                    if has(c):
                        rstd2.wait(dve, c)
                        moments2.wait(dve, c)
                        nc.vector.scalar_tensor_tensor(off2, mv2[:, :, 0], -1.0, r2, ALU.mult,
                                                       ALU.mult).then_inc(off2_ok.sem, 1)
                    if has(b):
                        for m in range(M):
                            scanned.wait(dve, b, m + 1)
                            evac.wait(dve, b, 2 * M + m + 1)
                            nc.vector.tensor_tensor(sg[:, m], sg[:, m], y[:, m], ALU.mult).then_inc(u_ok.sem, 1)
                    if has(c):
                        normed2.wait(dve, c)
                        cs_in.wait(dve, c)
                        nc.vector.tensor_tensor(h2, h2, mod_cs[:, 1:2].to_broadcast([P, J, C]),
                                                ALU.mult).then_inc(scaled2.sem, 1)
                    if has(a):
                        projected.wait(dve, a - 1)
                        nc.vector.tensor_copy(hl[:, :, 0:HW - T], pad_l[:, :, bass.ds(a, 1)].to_broadcast([P, M, HW - T])
                                              ).then_inc(h_lo.sem, 1)
                        for m in range(M):
                            h_hi.wait(dve, a, m + 2)
                            nc.vector.scalar_tensor_tensor(hl[:, m, HW - T:HW], tp[m][:], h_scale[:, m, bass.ds(a, 1)],
                                                           hh[:, m, HW - T:HW], ALU.mult,
                                                           ALU.subtract).then_inc(h_lo.sem, 1)
                    if has(b):
                        ssq_ok.wait(dve, b)
                        nc.vector.tensor_scalar(v4, ssq, S2 * S2 / (4 * C), S2 * S2 * EPS, ALU.mult,
                                                ALU.add).then_inc(rms_in.sem, 1)
                        for m in range(M):
                            u_hi.wait(dve, b, m + 1)
                            nc.vector.scalar_tensor_tensor(ul[:, m], sg[:, m], S, uh[:, m], ALU.mult,
                                                           ALU.subtract).then_inc(u_lo.sem, 1)
                    if has(c):
                        scored.wait(dve, c)
                        nc.vector.tensor_scalar(mean3, score[:, :, E], 1 / C, None, ALU.mult).then_inc(mean_ok.sem, 1)
                        nc.vector.tensor_scalar(v3, square, 1 / C, EPS, ALU.mult, ALU.add).then_inc(var3.sem, 1)
                        mean_ok.wait(dve, c)
                        nc.vector.tensor_tensor(mean3, mean3, mean3, ALU.mult).then_inc(mean_sq.sem, 1)
                        mean_sq.wait(dve, c)
                        var3.wait(dve, c, 1)
                        nc.vector.tensor_tensor(v3, v3, mean3, ALU.subtract).then_inc(var3.sem, 1)
                    if has(b):
                        rms_ok.wait(dve, b)
                        ga_in.wait(dve, b)
                        x1_ok.wait(dve, b - 1)
                        for j in range(J):
                            o_ok.wait(dve, b, j // 2 + 1)
                            nc.vector.scalar_tensor_tensor(attn[:, j], opj[j // 2][:, (j % 2) * C:(j % 2 + 1) * C],
                                                           rms[:, j:j + 1], mod_ga, ALU.mult,
                                                           ALU.mult).then_inc(attn_ok.sem, 1)
                    if has(c):
                        rstd3.wait(dve, c)
                        for j in range(J):
                            nc.vector.scalar_tensor_tensor(logit_b[:, j], score[:, j, 0:E], r3[:, j:j + 1],
                                                           gate_b[:], ALU.mult, ALU.add).then_inc(score_in.sem, 1)
                        for j in range(J):
                            score_in.wait(dve, c, j + 1)
                            settle()
                            nc.vector.max(top_b[:, j], logit_b[:, j]).then_inc(top_ok.sem, 1)
                        for j in range(J):
                            top_ok.wait(dve, c, j + 1)
                            settle()
                            nc.vector.max_index(picks[:, j], top_b[:, j], logit_b[:, j]).then_inc(picked.sem, 1)
                        nc.vector.tensor_copy(logits[:, bass.ds(c * J, J), :], logit_b).then_inc(kept.sem, 1)
                        nc.vector.tensor_copy(top[:, bass.ds(c * J, J), :], top_b[:, :, 0:2]).then_inc(kept.sem, 1)
                        picked.wait(dve, c)
                        for n in range(2):
                            nc.vector.tensor_copy(picks_f[:, n], picks[:, :, n]).then_inc(pick_f.sem, 1)
                        for n in range(2):
                            pick_f.wait(dve, c, n + 1)
                            nc.vector.tensor_tensor(
                                hot[:, n * J:(n + 1) * J], expert_id[:].unsqueeze(1).to_broadcast([P, J, E]),
                                picks_f[:, n].unsqueeze(2).to_broadcast([P, J, E]), ALU.is_equal).then_inc(hot_ok.sem, 1)
                        hot_ok.wait(dve, c)
                        nc.vector.tensor_tensor(hot2, hot[:, 0:J], hot[:, J:2 * J], ALU.add).then_inc(hot2_ok.sem, 1)
                        counted.wait(dve, c)
                        nc.vector.tensor_tensor(rank, ahead.rearrange("p (j e) -> p j e", e=E),
                                                base[:].unsqueeze(1).to_broadcast([P, J, E]),
                                                ALU.add).then_inc(rank_ok.sem, 1)
                        rank_ok.wait(dve, c)
                        nc.vector.tensor_tensor(base[:], base[:], total, ALU.add).then_inc(base_ok.sem, 1)
                        for n in range(2):
                            nc.vector.tensor_tensor(ranked_hot[:, n * J:(n + 1) * J], hot[:, n * J:(n + 1) * J], rank,
                                                    ALU.mult).then_inc(own_rank.sem, 1)
                        own_rank.wait(dve, c)
                        nc.vector.tensor_reduce(slots_f, ranked_hot, AX.X, ALU.add).then_inc(slot_f.sem, 1)
                        slot_f.wait(dve, c)
                        scattered.wait(dve, c - 1)
                        nc.vector.tensor_copy(slots_b, slots_f).then_inc(slot_ok.sem, 1)
                        nc.vector.tensor_copy(flat(slots[:, bass.ds(c, 1), :]), slots_f).then_inc(slot_ok.sem, 1)

                steps(dve, step)

            @block.tensor
            def _(pe):
                def project(a, p, m):
                    n = p * M + m
                    if n < M:
                        evac.wait(pe, a - 1, 3 * M + m + 1)
                    else:
                        evac.wait(pe, a, 2 * m + 2 if p == 1 else 2 * M + m + 1)
                    cols = slice(m * P, (m + 1) * P)
                    if p < 2:
                        ways = [(WPH[:, p, k, cols], WPL[:, p, k, cols], k, HW - T) for k in range(M)]
                    else:
                        ways = [(WFH[:, d, k, cols], WFL[:, d, k, cols], k, HW - T - (TAPS - 1) + d) for d in range(TAPS) for k in range(M)]
                    for i, (wh, wl, k, first) in enumerate(ways):
                        nc.tensor.matmul(prj[m][:], wh, hh[:, k, first:first + T], start=i == 0, stop=False)
                        nc.tensor.matmul(prj[m][:], wh, hl[:, k, first:first + T], start=False, stop=False)
                        last = nc.tensor.matmul(prj[m][:], wl, hh[:, k, first:first + T], start=False,
                                                stop=i == len(ways) - 1)
                    last.then_inc(projected.sem, 1)

                def step(t):
                    a, b, c = t + 1, t, t - 1
                    if has(a):
                        for m in range(M):
                            h2_sb.wait(pe, a - 3)
                            h_lo.wait(pe, a - 1)
                            for j in range(J):
                                normed.wait(pe, a, j + 1)
                                last = nc.tensor.transpose(tp[m][:, j * P:(j + 1) * P], xn[:, j, m * P:(m + 1) * P],
                                                           ident[:])
                            last.then_inc(xn_t.sem, 1)
                    if has(b):
                        rms_in.wait(pe, b - 1)
                        sq_ok.wait(pe, b)
                        for j in range(J):
                            for m in range(M):
                                last = nc.tensor.matmul(ssq[:, j:j + 1], sq[:, m, j * P:(j + 1) * P], ones[:, 0:1],
                                                        start=m == 0, stop=m == M - 1)
                        last.then_inc(ssq_ok.sem, 1)
                    if has(a):
                        h_lo.wait(pe, a)
                        for m in range(M):
                            project(a, 0, m)
                    if has(c):
                        if has(a):
                            h_lo.wait(pe, a)
                        for m in range(M):
                            h2_ok.wait(pe, c)
                            for j in range(J):
                                last = nc.tensor.transpose(tp[m][:, j * P:(j + 1) * P], h2[:, j, m * P:(m + 1) * P],
                                                           ident[:])
                            last.then_inc(h2_t.sem, 1)
                    if has(b):
                        attn_ok.wait(pe, b - 1)
                        u_lo.wait(pe, b)
                        for j in range(J):
                            dst = opj[j // 2][:, (j % 2) * C:(j % 2 + 1) * C]
                            tok = slice(j * P, (j + 1) * P)
                            for m in range(M):
                                nc.tensor.matmul(dst, uh[:, m, tok], WOH[:, m], start=m == 0, stop=False)
                                nc.tensor.matmul(dst, uh[:, m, tok], WOL[:, m], start=False, stop=False)
                                last = nc.tensor.matmul(dst, ul[:, m, tok], WOH[:, m], start=False, stop=m == M - 1)
                            if j % 2:
                                last.then_inc(o_ok.sem, 1)
                    if has(c):
                        h2_sb.wait(pe, c)
                        base_ok.wait(pe, c - 1)
                        rank_ok.wait(pe, c - 1)
                        for j in range(J):
                            for m in range(M):
                                nc.tensor.matmul(score[:, j], h2_tsb[:, m, j * P:(j + 1) * P], gate_c[:, m],
                                                 start=m == 0, stop=m == M - 1)
                        for j in range(J):
                            for m in range(M):
                                last = nc.tensor.matmul(square[:, j:j + 1], h2_sq[:, m, j * P:(j + 1) * P],
                                                        ones[:, 0:1], start=m == 0, stop=m == M - 1)
                        last.then_inc(scored.sem, 1)
                    if has(a):
                        for m in range(M):
                            project(a, 1, m)
                        project(a, 2, 0)
                    if has(c):
                        hot2_ok.wait(pe, c)
                        score_in.wait(pe, c)
                        for j in range(J):
                            for i in range(j + 1):
                                nc.tensor.matmul(ahead[:, j * E:(j + 1) * E], (before if i == j else ones16)[:],
                                                 hot2[:, i], start=i == 0, stop=i == j)
                        for j in range(J):
                            last = nc.tensor.matmul(total, ones16[:], hot2[:, j], start=j == 0, stop=j == J - 1)
                        last.then_inc(counted.sem, 1)
                    if has(a):
                        project(a, 2, 1)

                steps(pe, step)

        at = [0]
        zeros = place(at, [SUB, C])
        spread = place(at, [TILES, E])
        ratio = place(at, [TILES])
        denom = place(at, [TILES])
        table = [place(at, [LOOP_BLOCKS])[0:1] for _ in range(5)]
        number, inner, row, pick, extra = table
        cnt, nblk, cum, jump, rounded = (place(at, [E]) for _ in range(5))
        cnt_i = place(at, [E], I32)
        slot_y, past = place(at, [B * 2 * J]), place(at, [B * 2 * J])
        free_i = place(at, [E], I32)[0:1]
        from_row, which = (place(at, [LOOP_BLOCKS], I32)[0:1] for _ in range(2))
        xin = [place(at, [SUB, C]) for _ in range(2)]
        xh = [place(at, [M, BLK], F16) for _ in range(2)]
        xl = [place(at, [M, BLK], F16) for _ in range(2)]
        gel = [place(at, [FC, BLK]) for _ in range(2)]
        gh = [place(at, [FC, BLK], F16) for _ in range(2)]
        gl = [place(at, [FC, BLK], F16) for _ in range(2)]
        yo = [place(at, [SUB, C]) for _ in range(2)]
        xt_bank, y_bank = bank[0:2], bank[2:4]
        hid = [bank[4:6], bank[6:8]]

        iotas, table_dve, table_ok = sem("iotas"), sem("table_dve"), sem("table_ok")
        spread_ok, exp_ok = sem("spread_ok"), sem("exp_ok")
        padded = sem("padded")
        rows_in = [count(f"rows_in{s}", 16) for s in range(2)]
        y_out = [count(f"y_out{s}", 16) for s in range(2)]
        rows_t = count("rows_t", 1, 2)
        x_hi, x_lo = count("x_hi", 1, 2), count("x_lo", 1, 2)
        hid_ok = count("hid_ok", 2, 2)
        gelu_ok = count("gelu_ok", 2, 2)
        g_hi, g_lo = count("g_hi", 2, 2), count("g_lo", 2, 2)
        y_ok, y_sb = count("y_ok", 1, 2), count("y_sb", 1, 2)
        HALF = LOOP_BLOCKS // 2 - 1

        def pairs(eng, first, body, last):
            first()
            with eng.Fori(0, HALF) as q:
                body(q, 1)
                body(q, 2)
            last()

        with nc.Block() as block:

            @block.gpsimd
            def _(pool):
                nc.gpsimd.iota(number, pattern=[[1, LOOP_BLOCKS]], base=0, channel_multiplier=0,
                               allow_small_or_imprecise_dtypes=True).then_inc(iotas, 1)
                nc.gpsimd.memset(zeros, 0.0).then_inc(iotas, 1)

            @block.sync
            def _(sp):
                sp.wait_ge(table_ok, 3)
                sp.wait_ge(iotas, 2)
                for e in range(E):
                    first = sp.value_load(free_i[0:1, e:e + 1], min_val=0, max_val=E * REGION - BLK)
                    sp.dma_start(sorted_x[bass.ds(first, BLK), :].rearrange("(s p) c -> p s c", p=P),
                                 zeros).then_inc(padded, 16)
                sp.wait_ge(padded, 16 * E)

                def load(q, k):
                    sp.wait_ge(rows_t.sem, rows_t.at(2 * q + k - 2))
                    first = sp.value_load(from_row[0:1, bass.ds(2 * q + k, 1)], min_val=0, max_val=E * REGION - BLK)
                    sp.dma_start(xin[k % 2], sorted_x[bass.ds(first, BLK), :].rearrange("(s p) c -> p s c", p=P)
                                 ).then_inc(rows_in[k % 2].sem, 16)

                def store(q, k):
                    sp.wait_ge(y_sb.sem, y_sb.at(2 * q + k))
                    sp.dma_start(sorted_y[bass.ds((2 * q + k) * BLK, BLK), :].rearrange("(s p) c -> p s c", p=P), yo[k % 2]
                                 ).then_inc(y_out[k % 2].sem, 16)

                load(0, 0)
                load(0, 1)
                load(0, 2)
                with sp.Fori(0, HALF - 1) as q:
                    for k in (1, 2):
                        load(q, k + 2)
                        store(q, k - 1)
                load(HALF - 1, 3)
                store(HALF - 1, 0)
                store(HALF - 1, 1)
                store(HALF, 0)
                store(HALF, 1)
                for s in range(2):
                    sp.wait_ge(y_out[s].sem, 16 * LOOP_BLOCKS // 2)

            @block.scalar
            def _(act):
                act.sem_inc(x_hi.sem, 2)
                act.sem_inc(gelu_ok.sem, 4)
                act.sem_inc(y_sb.sem, 2)
                act.wait_ge(spread_ok, 2)
                nc.scalar.activation(flat(spread), flat(spread), ACT.Exp).then_inc(exp_ok, 1)
                nc.scalar.activation(ratio, ratio, ACT.Exp).then_inc(exp_ok, 1)
                nc.scalar.preload_act_table(ACT.Gelu)

                def high(q, k):
                    act.wait_ge(rows_t.sem, rows_t.at(2 * q + k))
                    act.wait_ge(hid_ok.sem, hid_ok.at(2 * q + k - 2))
                    nc.scalar.activation(flat(xh[k % 2]), xt_bank[k % 2][:], ACT.Copy, scale=S).then_inc(x_hi.sem, 1)

                def gelu(q, k):
                    for n in range(2):
                        act.wait_ge(hid_ok.sem, hid_ok.at(2 * q + k, n + 1))
                        act.wait_ge(g_lo.sem, g_lo.at(2 * q + k - 2))
                        nc.scalar.activation(flat(gel[k % 2][:, 2 * n:2 * n + 2]), hid[k % 2][n][:], ACT.Gelu,
                                             scale=1 / S2).then_inc(gelu_ok.sem, 1)

                def evacuate(q, k, reuse=True):
                    act.wait_ge(y_ok.sem, y_ok.at(2 * q + k))
                    if reuse:
                        act.wait_ge(y_out[k % 2].sem, y_out[k % 2].at(q + k // 2 - 1))
                    nc.scalar.activation(flat(yo[k % 2]), y_bank[k % 2][:], ACT.Copy, scale=1 / S2).then_inc(y_sb.sem, 1)

                high(0, 0)
                high(0, 1)
                gelu(0, 0)
                high(0, 2)
                gelu(0, 1)
                evacuate(0, 0, False)
                high(0, 3)
                gelu(0, 2)
                evacuate(0, 1, False)
                with act.Fori(1, HALF) as q:
                    for k in (1, 2):
                        high(q, k + 1)
                        gelu(q, k)
                        evacuate(q, k - 1)
                gelu(HALF, 1)
                evacuate(HALF, 0)
                evacuate(HALF, 1)

            @block.vector
            def _(dve):
                dve.sem_inc(x_lo.sem, 2)
                dve.sem_inc(g_hi.sem, 4)
                dve.sem_inc(g_lo.sem, 4)
                step = [0]

                def link(ins):
                    step[0] += 1
                    ins.then_inc(table_dve, 1)
                    dve.wait_ge(table_dve, step[0])

                link(nc.vector.scalar_tensor_tensor(cnt, expert_id[:], -float(REGION), base[:], ALU.mult, ALU.add))
                link(nc.vector.tensor_scalar(cnt_i, cnt, float(BLK - 1), None, ALU.add))
                link(nc.vector.tensor_scalar(cnt_i, cnt_i, BLK.bit_length() - 1, None, ALU.arith_shift_right))
                link(nc.vector.tensor_copy(nblk, cnt_i))
                link(nc.vector.memset(rounded, 0.0))
                link(nc.vector.tensor_tensor_scan(cum, nblk, rounded, 0.0, ALU.add, ALU.add))
                link(nc.vector.tensor_scalar(jump, nblk, -float(BLK), float(REGION), ALU.mult, ALU.add))
                last_block = cum[0:1, E - 1:E]
                dve.wait_ge(iotas, 2)
                link(nc.vector.tensor_scalar(rounded[0:1, 0:1], last_block, -1.0, None, ALU.add))
                link(nc.vector.tensor_scalar(inner, number, rounded[0:1, 0:1], None, ALU.min))
                link(nc.vector.tensor_scalar(row, inner, float(BLK), None, ALU.mult))
                link(nc.vector.tensor_scalar(pick, inner, 0.0, None, ALU.mult))
                for e in range(E - 1):
                    link(nc.vector.tensor_scalar(extra, inner, cum[0:1, e:e + 1], jump[0:1, e:e + 1], ALU.is_ge, ALU.mult))
                    link(nc.vector.tensor_tensor(row, row, extra, ALU.add))
                    link(nc.vector.scalar_tensor_tensor(pick, inner, cum[0:1, e:e + 1], pick, ALU.is_ge, ALU.add))
                nc.vector.tensor_copy(from_row, row).then_inc(table_ok, 1)
                nc.vector.tensor_copy(which, pick).then_inc(table_ok, 1)
                nc.vector.tensor_copy(free_i, base[0:1]).then_inc(table_ok, 1)
                nc.vector.tensor_tensor(spread, logits[:], top[:, :, 0:1].to_broadcast([P, TILES, E]),
                                        ALU.subtract).then_inc(spread_ok, 1)
                nc.vector.tensor_tensor(ratio, top[:, :, 1], top[:, :, 0], ALU.subtract).then_inc(spread_ok, 1)

                def low(q, k):
                    dve.wait_ge(x_hi.sem, x_hi.at(2 * q + k))
                    dve.wait_ge(hid_ok.sem, hid_ok.at(2 * q + k - 2))
                    nc.vector.scalar_tensor_tensor(flat(xl[k % 2]), xt_bank[k % 2][:], S, flat(xh[k % 2]), ALU.mult,
                                                   ALU.subtract).then_inc(x_lo.sem, 1)

                def split(q, k):
                    for n in range(2):
                        dve.wait_ge(gelu_ok.sem, gelu_ok.at(2 * q + k, n + 1))
                        dve.wait_ge(y_ok.sem, y_ok.at(2 * q + k - 2))
                        nc.vector.tensor_scalar(flat(gh[k % 2][:, 2 * n:2 * n + 2]), flat(gel[k % 2][:, 2 * n:2 * n + 2]),
                                                S, None, ALU.mult).then_inc(g_hi.sem, 1)
                    for n in range(2):
                        dve.wait_ge(g_hi.sem, g_hi.at(2 * q + k, n + 1))
                        nc.vector.scalar_tensor_tensor(
                            flat(gl[k % 2][:, 2 * n:2 * n + 2]), flat(gel[k % 2][:, 2 * n:2 * n + 2]), S,
                            flat(gh[k % 2][:, 2 * n:2 * n + 2]), ALU.mult, ALU.subtract).then_inc(g_lo.sem, 1)

                low(0, 0)
                low(0, 1)
                split(0, 0)
                with dve.Fori(0, HALF) as q:
                    for k in (1, 2):
                        low(q, k + 1)
                        split(q, k)
                split(HALF, 1)
                link(nc.vector.tensor_copy(slot_y, flat(slots[:])))
                for e in range(E - 1):
                    link(nc.vector.tensor_scalar(past, flat(slots[:]), float((e + 1) * REGION), jump[:, e:e + 1],
                                                 ALU.is_ge, ALU.mult))
                    link(nc.vector.tensor_tensor(slot_y, slot_y, past, ALU.subtract))
                link(nc.vector.tensor_copy(flat(slots[:]), slot_y))
                dve.wait_ge(exp_ok, 2)
                link(nc.vector.tensor_reduce(denom, spread, AX.X, ALU.add))
                link(nc.vector.reciprocal(prob[:, 0], denom))
                link(nc.vector.tensor_tensor(prob[:, 1], prob[:, 0], ratio, ALU.mult))

            @block.tensor
            def _(pe):
                pe.sem_inc(rows_t.sem, 2)
                pe.sem_inc(hid_ok.sem, 4)
                pe.sem_inc(y_ok.sem, 2)
                pe.wait_ge(table_ok, 3)

                def turn(q, k):
                    s = k % 2
                    pe.wait_ge(rows_in[s].sem, rows_in[s].at(q + k // 2))
                    pe.wait_ge(x_lo.sem, x_lo.at(2 * q + k - 2))
                    for m in range(M):
                        for t in range(SUB):
                            last = nc.tensor.transpose(xt_bank[s][:, m * BLK + t * P:m * BLK + (t + 1) * P],
                                                       xin[s][:, t, m * P:(m + 1) * P], ident[:])
                    last.then_inc(rows_t.sem, 1)

                def up(q, k):
                    s = k % 2
                    e = pe.value_load(which[0:1, bass.ds(2 * q + k, 1)], min_val=0, max_val=E - 1)
                    pe.wait_ge(x_lo.sem, x_lo.at(2 * q + k))
                    for n in range(2):
                        pe.wait_ge(gelu_ok.sem, gelu_ok.at(2 * q + k - 2, n + 1))
                        for i in range(2):
                            f = 2 * n + i
                            dst = hid[s][n][:, i * BLK:(i + 1) * BLK]
                            for m in range(M):
                                cols = bass.ds(e * F + (m * E * F + f * P), P)
                                nc.tensor.matmul(dst, WEH[:, cols], xh[s][:, m], start=m == 0, stop=False)
                                nc.tensor.matmul(dst, WEH[:, cols], xl[s][:, m], start=False, stop=False)
                                last = nc.tensor.matmul(dst, WEL[:, cols], xh[s][:, m], start=False, stop=m == M - 1)
                        last.then_inc(hid_ok.sem, 1)

                def down(q, k):
                    s = k % 2
                    e = pe.value_load(which[0:1, bass.ds(2 * q + k, 1)], min_val=0, max_val=E - 1)
                    pe.wait_ge(g_lo.sem, g_lo.at(2 * q + k))
                    pe.wait_ge(y_sb.sem, y_sb.at(2 * q + k - 2))
                    for t in range(SUB):
                        dst = y_bank[s][:, t * C:(t + 1) * C]
                        tok = slice(t * P, (t + 1) * P)
                        for f in range(FC):
                            cols = bass.ds(e * C + (W2_AT + f * E * C), C)
                            nc.tensor.matmul(dst, gh[s][:, f, tok], WEH[:, cols], start=f == 0, stop=False)
                            nc.tensor.matmul(dst, gh[s][:, f, tok], WEL[:, cols], start=False, stop=False)
                            last = nc.tensor.matmul(dst, gl[s][:, f, tok], WEH[:, cols], start=False, stop=f == FC - 1)
                    last.then_inc(y_ok.sem, 1)

                turn(0, 0)
                turn(0, 1)
                up(0, 0)
                with pe.Fori(0, HALF) as q:
                    for k in (1, 2):
                        turn(q, k + 1)
                        up(q, k)
                        down(q, k - 1)
                up(HALF, 1)
                down(HALF, 0)
                down(HALF, 1)

        at = [0]
        got = [place(at, [2 * J, C]) for _ in range(2)]
        mix = [place(at, [J, C]) for _ in range(2)]
        gain = [place(at, [C]) for _ in range(2)]
        index = [place(at, [2 * J], I32) for _ in range(2)]
        index_ok = count("index_ok", 1)
        gathered = [count(f"gathered{s}", 16 * 2 * J) for s in range(2)]
        gain_in = [count(f"gain_in{s}", 16) for s in range(2)]
        stored = [count(f"stored{s}", 16) for s in range(2)]
        first_ok, both_ok = count("first_ok", J), count("both_ok", J, 2)
        gained, summed = count("gained", 1), count("summed", 1, 2)

        with nc.Block() as block:

            @block.gpsimd
            def _(pool):
                def settle():
                    pool.sem_inc(pool_settled, 1)

                with pool.Fori(0, B // 2) as q:
                    for s in range(2):
                        b = 2 * q + s
                        pool.wait_ge(both_ok.sem, both_ok.at(b - 2))
                        settle()
                        nc.gpsimd.tensor_copy(index[s], flat(slots[:, bass.ds(b, 1), :])).then_inc(index_ok.sem, 1)
                        pool.wait_ge(index_ok.sem, index_ok.at(b))
                        settle()
                        for n in range(2 * J):
                            pool.indirect_dma_start(got[s][:, n], None, sorted_y, bass.IndirectOffsetOnAxis(
                                ap=index[s][:, n:n + 1], axis=0)).then_inc(gathered[s].sem, 16)

            @block.scalar
            def _(act):
                with act.Fori(0, B // 2) as q:
                    for s in range(2):
                        b = 2 * q + s
                        act.wait_ge(gathered[s].sem, gathered[s].at(q))
                        if s is not None:
                            act.wait_ge(summed.sem, summed.at(b - 2))
                        for j in range(J):
                            nc.scalar.activation(mix[s][:, j], got[s][:, j], ACT.Copy,
                                                 scale=prob[:, 0, bass.ds(b * J + j, 1)]).then_inc(first_ok.sem, 1)

            @block.vector
            def _(dve):
                dve.sem_inc(both_ok.sem, 2 * J)
                dve.sem_inc(summed.sem, 2)
                with dve.Fori(0, B // 2) as q:
                    for s in range(2):
                        b = 2 * q + s
                        dve.wait_ge(gathered[s].sem, gathered[s].at(q))
                        for j in range(J):
                            dve.wait_ge(first_ok.sem, first_ok.at(b, j + 1))
                            nc.vector.scalar_tensor_tensor(mix[s][:, j], got[s][:, J + j],
                                                           prob[:, 1, bass.ds(b * J + j, 1)], mix[s][:, j], ALU.mult,
                                                           ALU.add).then_inc(both_ok.sem, 1)
                        dve.wait_ge(both_ok.sem, both_ok.at(b))
                        dve.wait_ge(gain_in[s].sem, gain_in[s].at(q))
                        nc.vector.tensor_tensor(mix[s], mix[s], gain[s].unsqueeze(1).to_broadcast([P, J, C]),
                                                ALU.mult).then_inc(gained.sem, 1)
                        dve.wait_ge(gained.sem, gained.at(b))
                        xb = X[:, bass.ds(b * J, J), :]
                        nc.vector.tensor_tensor(xb, xb, mix[s], ALU.add).then_inc(summed.sem, 1)

            @block.sync
            def _(sp):
                with sp.Fori(0, B // 2) as q:
                    for s in range(2):
                        b = 2 * q + s
                        sp.wait_ge(summed.sem, summed.at(b - 2))
                        sp.dma_start(gain[s], mod_rows[bass.ds(b, 1), 3 * C:4 * C].to_broadcast([P, C])
                                     ).then_inc(gain_in[s].sem, 16)
                    for s in range(2):
                        b = 2 * q + s
                        sp.wait_ge(summed.sem, summed.at(b))
                        sp.dma_start(out[bass.ds(b * T, T), :].rearrange("(j p) c -> p j c", p=P),
                                     X[:, bass.ds(b * J, J), :]).then_inc(stored[s].sem, 16)
                for s in range(2):
                    sp.wait_ge(stored[s].sem, 16 * B // 2)


_IN = {
    "x": "L0_attn_x", "wi": "L0_attn_Wi", "wf": "L0_attn_Wf", "wg": "L0_attn_Wg", "conv_i": "L0_attn_conv_i",
    "conv_f": "L0_attn_conv_f", "gnorm": "L0_attn_g_norm_weight", "wo": "L0_attn_Wo", "gamma": "L0_ffn_ln_gamma",
    "beta": "L0_ffn_ln_beta", "gate": "L0_ffn_gate_w", "w1": "L0_ffn_w1", "w2": "L0_ffn_w2", "c_t": "L0_c",
    "wmod": "L0_wmod",
}


def lay_out(inputs):
    a = {k: np.asarray(inputs[v]) for k, v in _IN.items()}
    a["x"] = a["x"].reshape(N, C)
    for name in ("gnorm", "gamma", "beta"):
        a[name] = a[name].reshape(M, P).T
    a["gate"] = a["gate"].T
    a["c_t"] = a["c_t"].T
    a["conv_f_rows"] = a["conv_f"].T.reshape(1, TAPS * C)
    w1 = a.pop("w1").transpose(2, 0, 1).reshape(M, P, E * F // STAGE, STAGE).transpose(0, 2, 1, 3)
    w2 = a.pop("w2").transpose(2, 0, 1).reshape(FC, P, E * C // STAGE, STAGE).transpose(0, 2, 1, 3)
    a["w12"] = np.concatenate([w1.reshape(-1, STAGE), w2.reshape(-1, STAGE)])
    return {k: np.ascontiguousarray(v) for k, v in a.items()}


def kernel(**inputs):
    import concourse.bacc as bacc
    from concourse.bass_utils import run_bass_kernel_spmd

    nc = bacc.Bacc("TRN2", target_bir_lowering=False, num_devices=1)
    arrays = lay_out(inputs)
    aps = {k: nc.dram_tensor(f"in_{k}", a.shape, mybir.dt.from_np(a.dtype), kind="ExternalInput").ap()
           for k, a in arrays.items()}
    out = nc.dram_tensor("out_x", (N, C), F32, kind="ExternalOutput").ap()
    build(nc, out=out, **aps)
    got = run_bass_kernel_spmd(nc, [{f"in_{k}": a for k, a in arrays.items()}], core_ids=[0])
    return got.results[0]["out_x"].reshape(B, T, C)
```

```python
from contextlib import ExitStack

import numpy as np

import concourse.bass as bass
from concourse import mybir

F32, F16, I32, U32 = mybir.dt.float32, mybir.dt.float16, mybir.dt.int32, mybir.dt.uint32
ALU = mybir.AluOpType
ACT = mybir.ActivationFunctionType
AX = mybir.AxisListType

P = 128
B, T, C = 16, 512, 256
E, F = 8, 512
TAPS = 4
EPS = 1e-5
M = C // P
J = T // P
TILES = B * J
N = B * T
FC = F // P
BLK = 256
SUB = BLK // P
ROW = C + 2
REGION = N + BLK
BLOCKS = 2 * N // BLK + E - 1
SPARE = E - 1
ZW = TAPS - 1 + T
STAGE = (M * E * F + FC * E * C) // B
HW = ZW + 1
ARENA = 15056
S = 64.0
S2 = S * S


class Count:

    def __init__(self, sem, per, lead=0):
        self.sem, self.per, self.lead = sem, per, lead

    def at(self, rnd, n=None):
        n = self.per if n is None else n
        return rnd * self.per + (self.lead * self.per + n)

    def wait(self, eng, rnd, n=None):
        if not (isinstance(rnd, int) and rnd + self.lead < 0):
            eng.wait_ge(self.sem, self.at(rnd, n))


def build(nc, x, wi, wf, wg, conv_i, conv_f, conv_f_rows, gnorm, wo, gamma, beta, gate, w12, c_t, wmod, out):
    with ExitStack() as ctx:
        def sb(name, shape, dt=F32):
            return ctx.enter_context(nc.sbuf_tensor(name, shape, dt))

        def ps(name):
            return ctx.enter_context(nc.psum_tensor(name, [P, 512], F32))

        def sem(name):
            return ctx.enter_context(nc.semaphore(name))

        def count(name, per, lead=0):
            return Count(sem(name), per, lead)

        mod_rows = nc.dram_tensor("mod_rows", [B, 4 * C], F32, kind="Internal").ap()
        sorted_x = nc.dram_tensor("sorted_x", [E * REGION + SPARE * BLK, ROW], F32, kind="Internal").ap()
        expert_y = nc.dram_tensor("expert_y", [2 * N + (E + SPARE) * BLK, C], F32, kind="Internal").ap()

        X = sb("X", [P, TILES, C])
        WEH = sb("WEH", [P, B * STAGE], F16)
        WEL = sb("WEL", [P, B * STAGE], F16)
        W2_AT = M * E * F
        WPH = sb("WPH", [P, 2, M, C], F16)
        WPL = sb("WPL", [P, 2, M, C], F16)
        WFH = sb("WFH", [P, TAPS, M, C], F16)
        WFL = sb("WFL", [P, TAPS, M, C], F16)
        WOH = sb("WOH", [P, M, C], F16)
        WOL = sb("WOL", [P, M, C], F16)
        ident = sb("ident", [P, P])
        ones = sb("ones", [P, P])
        before = sb("before", [P, P], F16)
        ones16 = sb("ones16", [P, P], F16)
        expert_id = sb("expert_id", [P, E])
        number = sb("number", [P, BLOCKS])
        minus_half = sb("minus_half", [P, J])
        conv = sb("conv", [P, M, TAPS])
        h_scale = sb("h_scale", [P, M, B])
        bias = sb("bias", [P, 4, M, B])
        pad_h = sb("pad_h", [P, M, B], F16)
        pad_l = sb("pad_l", [P, M, B], F16)
        gate_c = sb("gate_c", [P, M, E])
        gate_b = sb("gate_b", [P, E])
        logits = sb("logits", [P, TILES, E])
        top = sb("top", [P, TILES, 2])
        tokens = sb("tokens", [P, J])
        scale_y = sb("scale_y", [P, M])
        prob = sb("prob", [P, 2, TILES])
        base = sb("base", [P, E])

        arena = sb("arena", [P, ARENA])

        def place(cursor, shape, dt=F32):
            n = int(np.prod(shape))
            words = n if dt != F16 else n // 2
            ap = arena[:, cursor[0]:cursor[0] + words]
            cursor[0] += words
            assert cursor[0] <= ARENA
            if dt != F32:
                ap = ap.bitcast(dt)
            if len(shape) == 2:
                ap = ap.rearrange("p (a b) -> p a b", b=shape[1])
            if len(shape) == 3:
                ap = ap.rearrange("p (a b c) -> p a b c", b=shape[1], c=shape[2])
            return ap

        bank = [ps(f"bank{n}") for n in range(8)]

        def flat(ap):
            return ap.rearrange("p a b -> p (a b)")

        at = [0]
        c_in = place(at, [M, B])
        silu_c = place(at, [M, B])
        shift_t = place(at, [M, B])
        w_mod = place(at, [M, 6 * C])
        w_in = place(at, [4, M * C])
        taps_f = place(at, [TAPS, C])
        w_tap = place(at, [TAPS, M * C])
        conv_fc = place(at, [M, TAPS])
        tap_sum = place(at, [M])
        norm_w = place(at, [M])
        gamma_c = place(at, [M])
        beta_c = place(at, [M])
        gate_t = place(at, [M, E])
        gate_gb = place(at, [M, 2 * E])
        rows_sb = place(at, [4, C])[0:B]
        sign_sb = place(at, [2, C])[0:B]
        KEPT_AT = ARENA - (J * C + J * 8 + 3 * J)
        assert at[0] <= KEPT_AT
        at = [KEPT_AT]
        xn = place(at, [J, C])
        bns1, mv1 = place(at, [J, 6]), place(at, [J, 2])
        r1, v1, off1 = (place(at, [J]) for _ in range(3))
        x_in, normed = count("x_in", 16), count("normed", J)
        stats1, moments1 = count("stats1", J), count("moments1", J)
        var1, rstd1, off1_ok = count("var1", 1), count("rstd1", 1), count("off1_ok", 1)

        def linker(eng, signal):
            step = [0]

            def link(ins):
                step[0] += 1
                ins.then_inc(signal, 1)
                eng.wait_ge(signal, step[0])
            return link

        consts = sem("consts")
        mod_in, small_in, w_loaded = sem("mod_in"), sem("small_in"), sem("w_loaded")
        SMALL, WEIGHTS = 7, 4
        c_ok, mod_ok, mod_sb, bias_ok, bias_sb = map(sem, ("c_ok", "mod_ok", "mod_sb", "bias_ok", "bias_sb"))
        gate_ok, gate_in = sem("gate_ok"), sem("gate_in")
        rows_ok, rows_out = sem("rows_ok"), sem("rows_out")
        wo_ok, tap_ok, split_hi = sem("wo_ok"), sem("tap_ok"), sem("split_hi")
        pad_ok = sem("pad_ok")
        setup_dve = sem("setup_dve")

        with nc.Block() as block:

            @block.sync
            def _(sp):
                sp.dma_start(X[:, 0:J, :], x[0:T, :].rearrange("(j p) c -> p j c", p=P)).then_inc(x_in.sem, 16)
                sp.dma_start(c_in, c_t.rearrange("(k p) b -> p k b", p=P)).then_inc(mod_in, 16)
                sp.dma_start(w_mod, wmod.rearrange("(k p) n -> p k n", p=P)).then_inc(mod_in, 16)
                for dst, src in (
                    (norm_w, gnorm), (gamma_c, gamma), (beta_c, beta), (gate_t, gate.rearrange("(m p) e -> p m e", p=P)),
                    (conv_fc, conv_f.rearrange("(m p) k -> p m k", p=P)),
                    (conv[:], conv_i.rearrange("(m p) k -> p m k", p=P)),
                    (taps_f.rearrange("p k c -> p (k c)"), conv_f_rows.to_broadcast([P, TAPS * C])),
                ):
                    sp.dma_start(dst, src).then_inc(small_in, 16)
                for n, w in enumerate((wi, wg, wf, wo)):
                    sp.dma_start(w_in[:, n].rearrange("p (k n) -> p k n", k=M), w.rearrange("(k p) n -> p k n", p=P)
                                 ).then_inc(w_loaded, 16)
                sp.wait_ge(rows_ok, 1)
                sp.dma_start(mod_rows.rearrange("b (q c) -> b q c", q=4), rows_sb).then_inc(rows_out, 16)
                sp.wait_ge(rows_out, 16)

            @block.gpsimd
            def _(pool):
                nc.gpsimd.memset(ident[:], 0.0).then_inc(consts, 1)
                nc.gpsimd.memset(ones[:], 1.0).then_inc(consts, 1)
                nc.gpsimd.memset(ones16[:], 1.0).then_inc(consts, 1)
                nc.gpsimd.memset(minus_half[:], -0.5).then_inc(consts, 1)
                nc.gpsimd.iota(expert_id[:], pattern=[[1, E]], base=0, channel_multiplier=0,
                               allow_small_or_imprecise_dtypes=True).then_inc(consts, 1)
                nc.gpsimd.iota(base[:], pattern=[[REGION, E]], base=0, channel_multiplier=0,
                               allow_small_or_imprecise_dtypes=True).then_inc(consts, 1)
                nc.gpsimd.iota(number[:], pattern=[[1, BLOCKS]], base=0, channel_multiplier=0,
                               allow_small_or_imprecise_dtypes=True).then_inc(consts, 1)
                nc.gpsimd.iota(tokens[:], pattern=[[P, J]], base=0, channel_multiplier=1,
                               allow_small_or_imprecise_dtypes=True).then_inc(consts, 1)
                pool.wait_ge(consts, 8)
                nc.gpsimd.affine_select(out=ident[:], in_=ident[:], compare_op=ALU.not_equal, fill=1.0,
                                        base=0, pattern=[[-1, P]], channel_multiplier=1).then_inc(consts, 1)
                nc.gpsimd.affine_select(out=before[:], in_=ones16[:], compare_op=ALU.is_gt, fill=0.0,
                                        base=0, pattern=[[1, P]], channel_multiplier=-1).then_inc(consts, 1)
                moments1.wait(pool, 0)
                nc.gpsimd.tensor_scalar(v1, mv1[:, :, 1], EPS, None, ALU.add).then_inc(var1.sem, 1)
                var1.wait(pool, 0)
                nc.gpsimd.tensor_tensor(r1, v1, minus_half[:], ALU.pow).then_inc(rstd1.sem, 1)
                pool.wait_ge(consts, 10)

            @block.scalar
            def _(act):
                nc.scalar.preload_act_table(ACT.Silu)
                off1_ok.wait(act, 0)
                rstd1.wait(act, 0)
                for j in range(J):
                    nc.scalar.activation(xn[:, j], X[:, j], ACT.Identity, scale=r1[:, j:j + 1],
                                         bias=off1[:, j:j + 1]).then_inc(normed.sem, 1)
                act.wait_ge(mod_in, 32)
                nc.scalar.activation(silu_c, c_in, ACT.Silu).then_inc(c_ok, 1)
                act.wait_ge(w_loaded, 16 * WEIGHTS)
                for n in range(2):
                    nc.scalar.activation(flat(WPH[:, n]), w_in[:, n], ACT.Copy, scale=S).then_inc(split_hi, 1)
                act.wait_ge(wo_ok, M)
                nc.scalar.activation(flat(WOH[:]), w_in[:, 3], ACT.Copy).then_inc(split_hi, 1)
                for k in range(TAPS):
                    act.wait_ge(tap_ok, M * (k + 1))
                    nc.scalar.activation(flat(WFH[:, k]), w_tap[:, k], ACT.Copy, scale=S).then_inc(split_hi, 1)
                act.wait_ge(mod_sb, 2)
                nc.scalar.activation(flat(pad_h[:]), flat(shift_t), ACT.Copy, scale=-S).then_inc(pad_ok, 1)

            @block.tensor
            def _(pe):
                pe.wait_ge(c_ok, 1)
                pe.wait_ge(mod_in, 32)
                for q in range(2 * M):
                    for k in range(M):
                        nc.tensor.matmul(bank[2][:, q * B:(q + 1) * B], w_mod[:, k, q * P:(q + 1) * P],
                                         silu_c[:, k], start=k == 0, stop=k == M - 1).then_inc(mod_ok, 1)
                for q in range(2):
                    for k in range(M):
                        nc.tensor.matmul(bank[q][0:B, :], silu_c[:, k],
                                         w_mod[:, k, (1 + q) * 2 * C:(2 + q) * 2 * C], start=k == 0,
                                         stop=k == M - 1).then_inc(mod_ok, 1)
                pe.wait_ge(mod_sb, 2)
                pe.wait_ge(w_loaded, 16 * WEIGHTS)
                for n in range(3 * M):
                    p, m = divmod(n, M)
                    for k in range(M):
                        nc.tensor.matmul(bank[3][:, n * B:(n + 1) * B], w_in[:, p, k * C + m * P:k * C + (m + 1) * P],
                                         shift_t[:, k], start=k == 0, stop=k == M - 1).then_inc(bias_ok, 1)
                pe.wait_ge(gate_in, 2 * M)
                pe.wait_ge(consts, 10)
                for k in range(M):
                    nc.tensor.matmul(bank[4][:, 0:2 * E], ones[:], gate_gb[:, k], start=k == 0,
                                     stop=k == M - 1).then_inc(gate_ok, 1)

            @block.vector
            def _(dve):
                link = linker(dve, setup_dve)

                x_in.wait(dve, 0)
                for j in range(J):
                    nc.vector.bn_stats(bns1[:, j], X[:, j]).then_inc(stats1.sem, 1)
                for j in range(J):
                    stats1.wait(dve, 0, j + 1)
                    nc.vector.bn_aggr(mv1[:, j], bns1[:, j]).then_inc(moments1.sem, 1)
                rstd1.wait(dve, 0)
                moments1.wait(dve, 0)
                nc.vector.scalar_tensor_tensor(off1, mv1[:, :, 0], -1.0, r1, ALU.mult,
                                               ALU.mult).then_inc(off1_ok.sem, 1)
                dve.wait_ge(small_in, 16 * SMALL)
                dve.wait_ge(w_loaded, 16 * WEIGHTS)
                for k in range(M):
                    nc.vector.tensor_scalar(gate_gb[:, k, 0:E], gate_t[:, k], gamma_c[:, k:k + 1], None,
                                            ALU.mult).then_inc(gate_in, 1)
                    nc.vector.tensor_scalar(gate_gb[:, k, E:2 * E], gate_t[:, k], beta_c[:, k:k + 1], None,
                                            ALU.mult).then_inc(gate_in, 1)
                for k in range(M):
                    nc.vector.tensor_scalar(w_in[:, 3, k * C:(k + 1) * C], w_in[:, 3, k * C:(k + 1) * C],
                                            norm_w[:, k:k + 1], -0.5 * S, ALU.mult, ALU.mult).then_inc(wo_ok, 1)
                for k in range(TAPS):
                    for m in range(M):
                        cols = slice(m * C, (m + 1) * C)
                        nc.vector.tensor_tensor(w_tap[:, k, cols], w_in[:, 2, cols], taps_f[:, k],
                                                ALU.mult).then_inc(tap_ok, 1)
                link(nc.vector.tensor_reduce(tap_sum, conv_fc, AX.X, ALU.add))
                dve.wait_ge(mod_ok, 2 * M * M)
                nc.vector.tensor_copy(flat(shift_t), bank[2][:, 0:M * B]).then_inc(mod_sb, 1)
                nc.vector.tensor_scalar(flat(h_scale[:]), bank[2][:, M * B:2 * M * B], 1.0, S, ALU.add,
                                        ALU.mult).then_inc(mod_sb, 1)
                dve.wait_ge(split_hi, 2)
                for n in range(2):
                    nc.vector.scalar_tensor_tensor(flat(WPL[:, n]), w_in[:, n], S, flat(WPH[:, n]), ALU.mult,
                                                   ALU.subtract).then_inc(bias_sb, 1)
                dve.wait_ge(split_hi, 3)
                dve.wait_ge(wo_ok, M)
                nc.vector.tensor_tensor(flat(WOL[:]), w_in[:, 3], flat(WOH[:]), ALU.subtract).then_inc(bias_sb, 1)
                dve.wait_ge(tap_ok, M * TAPS)
                for k in range(TAPS):
                    dve.wait_ge(split_hi, 4 + k)
                    nc.vector.scalar_tensor_tensor(flat(WFL[:, k]), w_tap[:, k], S, flat(WFH[:, k]), ALU.mult,
                                                   ALU.subtract).then_inc(bias_sb, 1)
                dve.wait_ge(mod_ok, 2 * M + 2 * M * M)
                for q, r, first in ((0, 0, 0), (1, 3, C)):
                    gain = bank[q][0:B, first:first + C]
                    link(nc.vector.tensor_scalar(sign_sb[:, 0], gain, 0.0, 2.0, ALU.is_ge, ALU.mult))
                    link(nc.vector.tensor_scalar(sign_sb[:, 1], gain, -1.0, 0.25, ALU.mult, ALU.max))
                    link(nc.vector.tensor_tensor(sign_sb[:, 1], sign_sb[:, 1], gain, ALU.max))
                    link(nc.vector.scalar_tensor_tensor(rows_sb[:, r], sign_sb[:, 0], -1.0, sign_sb[:, 1],
                                                        ALU.add, ALU.mult))
                link(nc.vector.tensor_copy(rows_sb[:, 1], bank[0][0:B, C:2 * C]))
                nc.vector.tensor_scalar(rows_sb[:, 2], bank[1][0:B, 0:C], 1.0, None, ALU.add).then_inc(rows_ok, 1)
                dve.wait_ge(pad_ok, 1)
                nc.vector.scalar_tensor_tensor(flat(pad_l[:]), flat(shift_t), -S, flat(pad_h[:]), ALU.mult,
                                               ALU.subtract).then_inc(bias_sb, 1)
                dve.wait_ge(bias_ok, 3 * M * M)
                sums = bank[3][:, 0:3 * M * B].rearrange("p (n m b) -> p n m b", n=3, m=M)
                link(nc.vector.tensor_copy(bias[:, 0:2].rearrange("p n m b -> p (n m b)"), bank[3][:, 0:2 * M * B]))
                for m in range(M):
                    nc.vector.tensor_scalar(bias[:, 2, m], sums[:, 2, m], tap_sum[:, m:m + 1], 0.5, ALU.mult,
                                            ALU.mult).then_inc(bias_sb, 1)
                    nc.vector.tensor_scalar(bias[:, 3, m], sums[:, 0, m], conv[:, m, TAPS - 1:TAPS], None,
                                            ALU.mult).then_inc(bias_sb, 1)
                nc.vector.tensor_scalar(scale_y[:], conv[:, :, TAPS - 1], 1 / S2, None, ALU.mult).then_inc(bias_sb, 1)
                dve.wait_ge(gate_ok, M)
                dve.wait_ge(gate_in, 2 * M)
                nc.vector.tensor_copy(gate_b[:], bank[4][:, E:2 * E]).then_inc(bias_sb, 1)
                for k in range(M):
                    nc.vector.scalar_tensor_tensor(gate_c[:, k, 0:E], bank[4][:, 0:E], -1.0 / C, gate_gb[:, k, 0:E],
                                                   ALU.mult, ALU.add).then_inc(bias_sb, 1)

        at = [0]
        hh, hl = place(at, [M, HW], F16), place(at, [M, HW], F16)
        z = place(at, [M, ZW])
        y = place(at, [M, T])
        sg = place(at, [M, T])
        th = place(at, [M, T])
        sq = place(at, [M, T])
        attn = place(at, [J, C])
        uh, ul = place(at, [M, T], F16), place(at, [M, T], F16)
        mixer_end = at[0]
        mod_ga = place(at, [C])
        mod_cs = place(at, [2, C])
        h2_tsb = place(at, [M, T])
        w_stage = place(at, [STAGE])
        dead_end = at[0]
        h2 = [place(at, [J, ROW]) for _ in range(2)]
        bns2, bns3 = (place(at, [J, 6]) for _ in range(2))
        mv2, mv3 = (place(at, [J, 2]) for _ in range(2))
        r2, r3, rms = (place(at, [J]) for _ in range(3))
        v2, v3, v4 = (place(at, [J]) for _ in range(3))
        off2 = place(at, [J])
        picks = place(at, [J, 8], U32)
        picks_f = place(at, [2, J])
        hot = place(at, [2 * J, E])
        ranked_hot = place(at, [2 * J, E])
        hot2 = place(at, [J, E], F16)
        rank = place(at, [J, E])
        logit_b, top_b = place(at, [J, E]), place(at, [J, E])
        slots_f = place(at, [2 * J])
        slots_b = place(at, [2 * J], I32)
        assert at[0] <= KEPT_AT
        tp, prj = bank[0:2], bank[2:4]
        opj = bank[4:6]
        ssq = bank[6][:, 0:J]
        score = bank[7][:, 0:J * E].rearrange("p (j e) -> p j e", e=E)
        ahead = bank[7][:, 64:64 + J * E]
        total = bank[7][:, 128:128 + E]

        SOON, LATE = 2, 5

        at = [0]
        padding = place(at, [(E + SPARE) * SUB, ROW])
        after_padding = at[0]
        assert at[0] <= mixer_end
        spread = place(at, [TILES, E])
        ratio = place(at, [TILES])
        denom = place(at, [TILES])
        skipped, row, which_f = (place(at, [BLOCKS]) for _ in range(3))
        reached, jumps = place(at, [BLOCKS, E]), place(at, [BLOCKS, E])
        cnt, nblk, cum, jump, no = (place(at, [E]) for _ in range(5))
        cnt_i = place(at, [E], I32)
        free_i = place(at, [E], I32)[0:1]
        from_row, which = (place(at, [BLOCKS], I32)[0:1] for _ in range(2))
        assert at[0] <= dead_end
        table_dve, table_ok, padding_ok, padded = map(sem, ("table_dve", "table_ok", "padding_ok", "padded"))
        zeroed, free_ok = sem("zeroed"), sem("free_ok")

        pads = sem("pads")
        dve_settled, pool_settled = sem("dve_settled"), sem("pool_settled")
        ga_in, cs_in, stage_in = count("ga_in", 16), count("cs_in", 16), count("stage_in", 16)
        stage_scaled, stage_lo = count("stage_scaled", 2), count("stage_lo", 1)
        xn_t = count("xn_t", M)
        h_hi, h_lo = count("h_hi", M + 1), count("h_lo", M + 1)
        projected = count("projected", 6)
        evac = count("evac", 8)
        conv_ok = count("conv_ok", M * (TAPS - 1))
        silu_i, forget_ok, gate_i = count("silu_i", M), count("forget_ok", M), count("gate_i", M)
        scanned = count("scanned", M)
        sq_ok, ssq_ok = count("sq_ok", M), count("ssq_ok", 1)
        rms_in, rms_ok = count("rms_in", 1), count("rms_ok", 1)
        u_ok, u_hi, u_lo = count("u_ok", M), count("u_hi", M), count("u_lo", M)
        o_ok = count("o_ok", 2)
        attn_ok = count("attn_ok", J)
        x1_ok = count("x1_ok", 1)
        stats2, moments2 = count("stats2", J), count("moments2", J)
        var2, rstd2, off2_ok = count("var2", 1), count("rstd2", 1), count("off2_ok", 1)
        normed2, scaled2, h2_ok = count("normed2", J), count("scaled2", 1), count("h2_ok", 1)
        h2_t, h2_sb = count("h2_t", M), count("h2_sb", M)
        stats3, moments3 = count("stats3", J), count("moments3", J)
        scored, var3, rstd3 = count("scored", 1), count("var3", 1), count("rstd3", 1)
        score_in, top_ok, picked = count("score_in", J), count("top_ok", J), count("picked", J)
        kept, pick_f = count("kept", 2), count("pick_f", 2)
        hot_ok, hot2_ok = count("hot_ok", 2), count("hot2_ok", 1)
        counted, rank_ok, base_ok = count("counted", 1), count("rank_ok", 1), count("base_ok", 1)
        own_rank, slot_f, slot_ok = count("own_rank", 2), count("slot_f", 1), count("slot_ok", 1)
        tagged = count("tagged", 3)
        scattered = count("scattered", 16 * 2 * J)

        def steps(eng, step, ahead=2, behind=1):
            for t in range(-1, 2 * behind):
                step(t, t % 2)
            with eng.Fori(behind, (B - ahead) // 2) as half:
                for s in range(2):
                    step(2 * half + s, s)
            for t in range(B - ahead, B + 2):
                step(t, t % 2)

        def has(n):
            return not isinstance(n, int) or 0 <= n < B

        with nc.Block() as block:

            @block.sync
            def _(sp):
                def step(t, s):
                    n, a, b, c = t + 2, t + 1, t, t - 1
                    if has(t + 3):
                        x_in.wait(sp, n)
                        sp.dma_start(X[:, bass.ds((t + 3) * J, J), :],
                                     x[bass.ds((t + 3) * T, T), :].rearrange("(j p) c -> p j c", p=P)
                                     ).then_inc(x_in.sem, 16)
                    if has(a):
                        stage_lo.wait(sp, b)
                        stage_in.wait(sp, b)
                        sp.dma_start(w_stage, w12[bass.ds(a * P, P), :]).then_inc(stage_in.sem, 16)
                        attn_ok.wait(sp, b)
                        ga_in.wait(sp, b)
                        sp.dma_start(mod_ga, mod_rows[bass.ds(a, 1), 0:C].to_broadcast([P, C])
                                     ).then_inc(ga_in.sem, 16)
                    if has(b):
                        h2_ok.wait(sp, b - 1)
                        cs_in.wait(sp, b - 1)
                        sp.dma_start(mod_cs.rearrange("p q c -> p (q c)"),
                                     mod_rows[bass.ds(b, 1), C:3 * C].to_broadcast([P, 2 * C])
                                     ).then_inc(cs_in.sem, 16)

                sp.dma_start(X[:, J:2 * J, :], x[T:2 * T, :].rearrange("(j p) c -> p j c", p=P)
                             ).then_inc(x_in.sem, 16)
                steps(sp, step, ahead=4)
                sp.wait_ge(padding_ok, 2)
                sp.dma_start(sorted_x[E * REGION:E * REGION + SPARE * BLK, :].rearrange("(s p) c -> p s c", p=P),
                             padding[:, E * SUB:(E + SPARE) * SUB]).then_inc(padded, 16)
                sp.wait_ge(free_ok, 1)
                for e in range(E):
                    first = sp.value_load(free_i[0:1, e:e + 1], min_val=0, max_val=E * REGION - BLK)
                    sp.dma_start(sorted_x[bass.ds(first, BLK), :].rearrange("(s p) c -> p s c", p=P),
                                 padding[:, e * SUB:(e + 1) * SUB]).then_inc(padded, 16)
                sp.wait_ge(padded, 16 * (E + 1))

            @block.gpsimd
            def _(pool):
                def settle():
                    pool.sem_inc(pool_settled, 1)

                def rstd(n, moments, mv, v, var, r, ok):
                    moments.wait(pool, n)
                    settle()
                    nc.gpsimd.tensor_scalar(v, mv[:, :, 1], EPS, None, ALU.add).then_inc(var.sem, 1)
                    var.wait(pool, n)
                    nc.gpsimd.tensor_tensor(r, v, minus_half[:], ALU.pow).then_inc(ok.sem, 1)

                def step(t, s):
                    n, a, b, c, d = t + 2, t + 1, t, t - 1, t - 2

                    def scatter(buffer, pieces):
                        for i in pieces:
                            pool.indirect_dma_start(sorted_x, bass.IndirectOffsetOnAxis(ap=slots_b[:, i:i + 1], axis=0),
                                                    buffer[:, i % J], None).then_inc(scattered.sem, 16)

                    if has(b):
                        rms_in.wait(pool, b)
                        nc.gpsimd.tensor_tensor(rms, v4, minus_half[:], ALU.pow).then_inc(rms_ok.sem, 1)
                    if has(c):
                        scaled2.wait(pool, c)
                        cs_in.wait(pool, c)
                        rows = h2[1 - s][:, :, 0:C]
                        nc.gpsimd.tensor_tensor(rows, rows, mod_cs[:, 0:1].to_broadcast([P, J, C]),
                                                ALU.add).then_inc(h2_ok.sem, 1)
                    if has(d):
                        slot_ok.wait(pool, d)
                        tagged.wait(pool, d)
                        settle()
                        scatter(h2[s], range(SOON))
                    if has(b):
                        attn_ok.wait(pool, b)
                        settle()
                        xb = X[:, bass.ds(b * J, J), :]
                        nc.gpsimd.tensor_tensor(xb, xb, attn, ALU.add).then_inc(x1_ok.sem, 1)
                    if has(n):
                        rstd(n, moments1, mv1, v1, var1, r1, rstd1)
                    if has(d):
                        scatter(h2[s], range(SOON, LATE))
                    if has(c):
                        rstd(c, moments3, mv3, v3, var3, r3, rstd3)
                    if has(b):
                        rstd(b, moments2, mv2, v2, var2, r2, rstd2)
                    if has(d):
                        scatter(h2[s], range(LATE, 2 * J))
                    if has(b):
                        stage_scaled.wait(pool, b)
                        settle()
                        cols = bass.ds(b * STAGE, STAGE)
                        nc.gpsimd.tensor_tensor(WEL[:, cols], w_stage, WEH[:, cols],
                                                ALU.subtract).then_inc(stage_lo.sem, 1)

                steps(pool, step)
                scattered.wait(pool, B - 1)

            @block.scalar
            def _(act):
                def square(n, m):
                    scanned.wait(act, n, m + 1)
                    ssq_ok.wait(act, n - 1)
                    nc.scalar.activation(sq[:, m], y[:, m], ACT.Square).then_inc(sq_ok.sem, 1)

                def step(t, s):
                    n, a, b, c = t + 2, t + 1, t, t - 1

                    def normalise(j):
                        nc.scalar.activation(h2[1 - s][:, j, 0:C], flat(X[:, bass.ds(c * J + j, 1), :]), ACT.Identity,
                                             scale=r2[:, j:j + 1], bias=off2[:, j:j + 1]).then_inc(normed2.sem, 1)

                    def silu_g(m):
                        projected.wait(act, b, 2 * M + m + 1)
                        u_lo.wait(act, b - 1)
                        nc.scalar.activation(sg[:, m], prj[m][:], ACT.Silu, scale=1 / S2,
                                             bias=bias[:, 1, m, bass.ds(b, 1)]).then_inc(evac.sem, 1)

                    if has(b):
                        silu_g(0)
                    if has(c):
                        off2_ok.wait(act, c)
                        rstd2.wait(act, c)
                        scattered.wait(act, c - 2)
                        for j in range(J // 2):
                            normalise(j)
                    if has(b):
                        silu_g(1)
                        square(b, 1)
                        for m in range(M):
                            u_ok.wait(act, b, m + 1)
                            o_ok.wait(act, b - 1)
                            nc.scalar.activation(uh[:, m], sg[:, m], ACT.Copy, scale=S).then_inc(u_hi.sem, 1)
                    if has(a):
                        projected.wait(act, a - 1)
                        nc.scalar.activation(hh[:, :, 0:HW - T], pad_h[:, :, bass.ds(a, 1)].to_broadcast([P, M, HW - T]),
                                             ACT.Copy).then_inc(h_hi.sem, 1)
                        for m in range(M):
                            xn_t.wait(act, a, m + 1)
                            nc.scalar.activation(hh[:, m, HW - T:HW], tp[m][:], ACT.Copy,
                                                 scale=h_scale[:, m, bass.ds(a, 1)]).then_inc(h_hi.sem, 1)
                    if has(c):
                        for j in range(J // 2, J):
                            normalise(j)
                    if has(b):
                        stage_in.wait(act, b)
                        nc.scalar.activation(WEH[:, bass.ds(b * STAGE, STAGE)], w_stage, ACT.Copy,
                                             scale=S).then_inc(stage_scaled.sem, 1)
                        nc.scalar.activation(w_stage, w_stage, ACT.Copy, scale=S).then_inc(stage_scaled.sem, 1)
                    if has(a):
                        for m in range(M):
                            projected.wait(act, a, m + 1)
                            conv_ok.wait(act, a - 1)
                            nc.scalar.activation(z[:, m, ZW - T:ZW], prj[m][:], ACT.Identity, scale=1 / S2,
                                                 bias=bias[:, 0, m, bass.ds(a, 1)]).then_inc(evac.sem, 1)
                            u_ok.wait(act, a - 1)
                            sq_ok.wait(act, a - 1)
                            nc.scalar.activation(y[:, m], prj[m][:], ACT.Identity, scale=scale_y[:, m:m + 1],
                                                 bias=bias[:, 3, m, bass.ds(a, 1)]).then_inc(evac.sem, 1)
                    if has(c):
                        for m in range(M):
                            h2_t.wait(act, c, m + 1)
                            scored.wait(act, c - 1)
                            nc.scalar.activation(h2_tsb[:, m], tp[m][:], ACT.Copy).then_inc(h2_sb.sem, 1)
                    if has(n):
                        off1_ok.wait(act, n)
                        rstd1.wait(act, n)
                        xn_t.wait(act, a)
                        for j in range(J):
                            nc.scalar.activation(xn[:, j], flat(X[:, bass.ds(n * J + j, 1), :]), ACT.Identity,
                                                 scale=r1[:, j:j + 1], bias=off1[:, j:j + 1]).then_inc(normed.sem, 1)

                    def tanh(m):
                        projected.wait(act, a, M + m + 1)
                        scanned.wait(act, a - 1, m + 1)
                        nc.scalar.activation(th[:, m], opj[m][:], ACT.Tanh, scale=0.5 / S2,
                                             bias=bias[:, 2, m, bass.ds(a, 1)]).then_inc(evac.sem, 1)

                    if has(a):
                        tanh(0)
                        for m in range(M):
                            conv_ok.wait(act, a, M * (TAPS - 2) + m + 1)
                            nc.scalar.activation(y[:, m], y[:, m], ACT.Silu).then_inc(silu_i.sem, 1)
                    if has(a):
                        square(a, 0)
                        tanh(1)

                steps(act, step, behind=2)

            @block.vector
            def _(dve):
                nc.vector.memset(z[:, :, 0:ZW - T], 0.0).then_inc(pads, 1)
                dve.wait_ge(pads, 1)

                def settle():
                    dve.sem_inc(dve_settled, 1)

                def statistics(n, row, ready, bns, stats, mv, moments):
                    ready.wait(dve, n)
                    settle()
                    for j in range(J):
                        nc.vector.bn_stats(bns[:, j], row(j)).then_inc(stats.sem, 1)
                    for j in range(J):
                        stats.wait(dve, n, j + 1)
                        settle()
                        nc.vector.bn_aggr(mv[:, j], bns[:, j]).then_inc(moments.sem, 1)

                def recurrence(n, m):
                    silu_i.wait(dve, n, m + 1)
                    evac.wait(dve, n, 2 * M + m + 1)
                    nc.vector.scalar_tensor_tensor(y[:, m], th[:, m], -1.0, y[:, m], ALU.add,
                                                   ALU.mult).then_inc(gate_i.sem, 1)
                    gate_i.wait(dve, n, m + 1)
                    nc.vector.tensor_scalar(th[:, m], th[:, m], 0.5, 0.5, ALU.mult,
                                            ALU.add).then_inc(forget_ok.sem, 1)
                    forget_ok.wait(dve, n, m + 1)
                    nc.vector.tensor_tensor_scan(y[:, m], th[:, m], y[:, m], 0.0, ALU.mult,
                                                 ALU.add).then_inc(scanned.sem, 1)

                def clear_padding(half):
                    x1_ok.wait(dve, B - 1)
                    tiles = (E + SPARE) * SUB // 2
                    nc.vector.memset(padding[:, half * tiles:(half + 1) * tiles], 0.0).then_inc(zeroed, 1)

                def step(t, s):
                    n, a, b, c, d = t + 2, t + 1, t, t - 1, t - 2
                    last_routed = isinstance(t, int) and t == B
                    if last_routed:
                        clear_padding(0)
                    if has(b):
                        recurrence(b, 1)
                        for m in range(M):
                            scanned.wait(dve, b, m + 1)
                            evac.wait(dve, b, 3 * M + m + 1)
                            nc.vector.tensor_tensor(sg[:, m], sg[:, m], y[:, m], ALU.mult).then_inc(u_ok.sem, 1)
                    if has(b):
                        for m in range(M):
                            u_hi.wait(dve, b, m + 1)
                            nc.vector.scalar_tensor_tensor(ul[:, m], sg[:, m], S, uh[:, m], ALU.mult,
                                                           ALU.subtract).then_inc(u_lo.sem, 1)
                    if has(b):
                        ssq_ok.wait(dve, b)
                        nc.vector.tensor_scalar(v4, ssq, S2 * S2 / (4 * C), S2 * S2 * EPS, ALU.mult,
                                                ALU.add).then_inc(rms_in.sem, 1)
                    if has(a):
                        projected.wait(dve, a - 1)
                        nc.vector.tensor_copy(hl[:, :, 0:HW - T], pad_l[:, :, bass.ds(a, 1)].to_broadcast([P, M, HW - T])
                                              ).then_inc(h_lo.sem, 1)
                        for m in range(M):
                            h_hi.wait(dve, a, m + 2)
                            nc.vector.scalar_tensor_tensor(hl[:, m, HW - T:HW], tp[m][:], h_scale[:, m, bass.ds(a, 1)],
                                                           hh[:, m, HW - T:HW], ALU.mult,
                                                           ALU.subtract).then_inc(h_lo.sem, 1)
                    if has(c):
                        normed2.wait(dve, c)
                        cs_in.wait(dve, c)
                        rows = h2[1 - s][:, :, 0:C]
                        nc.vector.tensor_tensor(rows, rows, mod_cs[:, 1:2].to_broadcast([P, J, C]),
                                                ALU.mult).then_inc(scaled2.sem, 1)
                    if has(d):
                        counted.wait(dve, d)
                        nc.vector.tensor_tensor(rank, ahead.rearrange("p (j e) -> p j e", e=E),
                                                base[:].unsqueeze(1).to_broadcast([P, J, E]),
                                                ALU.add).then_inc(rank_ok.sem, 1)
                        rank_ok.wait(dve, d)
                        nc.vector.tensor_tensor(base[:], base[:], total, ALU.add).then_inc(base_ok.sem, 1)
                        for i in range(2):
                            nc.vector.tensor_tensor(ranked_hot[:, i * J:(i + 1) * J], hot[:, i * J:(i + 1) * J], rank,
                                                    ALU.mult).then_inc(own_rank.sem, 1)
                        own_rank.wait(dve, d)
                        nc.vector.tensor_reduce(slots_f, ranked_hot, AX.X, ALU.add).then_inc(slot_f.sem, 1)
                        slot_f.wait(dve, d)
                        scattered.wait(dve, d - 1)
                        nc.vector.tensor_copy(slots_b, slots_f).then_inc(slot_ok.sem, 1)
                    if has(b):
                        rms_ok.wait(dve, b)
                        ga_in.wait(dve, b)
                        x1_ok.wait(dve, b - 1)
                        for j in range(J):
                            o_ok.wait(dve, b, j // 2 + 1)
                            nc.vector.scalar_tensor_tensor(attn[:, j], opj[j // 2][:, (j % 2) * C:(j % 2 + 1) * C],
                                                           rms[:, j:j + 1], mod_ga, ALU.mult,
                                                           ALU.mult).then_inc(attn_ok.sem, 1)
                    if has(n):
                        statistics(n, lambda j: flat(X[:, bass.ds(n * J + j, 1), :]), x_in, bns1, stats1, mv1, moments1)
                    if has(a):
                        for k in range(1, TAPS):
                            for m in range(M):
                                if k == 1:
                                    evac.wait(dve, a, 2 * m + 2)
                                else:
                                    conv_ok.wait(dve, a, (k - 2) * M + m + 1)
                                nc.vector.scalar_tensor_tensor(
                                    y[:, m], z[:, m, ZW - T - k:ZW - k], conv[:, m, TAPS - 1 - k:TAPS - k],
                                    y[:, m], ALU.mult, ALU.add).then_inc(conv_ok.sem, 1)
                    if has(n):
                        rstd1.wait(dve, n)
                        moments1.wait(dve, n)
                        nc.vector.scalar_tensor_tensor(off1, mv1[:, :, 0], -1.0, r1, ALU.mult,
                                                       ALU.mult).then_inc(off1_ok.sem, 1)
                    if has(c):
                        statistics(c, lambda j: h2[1 - s][:, j, 0:C], h2_ok, bns3, stats3, mv3, moments3)
                    if has(b):
                        statistics(b, lambda j: flat(X[:, bass.ds(b * J + j, 1), :]), x1_ok, bns2, stats2, mv2, moments2)
                    if has(a):
                        recurrence(a, 0)
                    if last_routed:
                        clear_padding(1)
                    if has(c):
                        scored.wait(dve, c)
                        rstd3.wait(dve, c)
                        for j in range(J):
                            nc.vector.scalar_tensor_tensor(logit_b[:, j], score[:, j], r3[:, j:j + 1],
                                                           gate_b[:], ALU.mult, ALU.add).then_inc(score_in.sem, 1)
                        for j in range(J):
                            score_in.wait(dve, c, j + 1)
                            settle()
                            nc.vector.max(top_b[:, j], logit_b[:, j]).then_inc(top_ok.sem, 1)
                        for j in range(J):
                            top_ok.wait(dve, c, j + 1)
                            settle()
                            nc.vector.max_index(picks[:, j], top_b[:, j], logit_b[:, j]).then_inc(picked.sem, 1)
                        picked.wait(dve, c)
                        for i in range(2):
                            nc.vector.tensor_copy(picks_f[:, i], picks[:, :, i]).then_inc(pick_f.sem, 1)
                        for i in range(2):
                            pick_f.wait(dve, c, i + 1)
                            nc.vector.tensor_tensor(
                                hot[:, i * J:(i + 1) * J], expert_id[:].unsqueeze(1).to_broadcast([P, J, E]),
                                picks_f[:, i].unsqueeze(2).to_broadcast([P, J, E]), ALU.is_equal).then_inc(hot_ok.sem, 1)
                        hot_ok.wait(dve, c)
                        nc.vector.tensor_tensor(hot2, hot[:, 0:J], hot[:, J:2 * J], ALU.add).then_inc(hot2_ok.sem, 1)
                        tagged.wait(dve, c - 1)
                        nc.vector.tensor_copy(h2[1 - s][:, :, C], tokens[:]).then_inc(tagged.sem, 1)
                        nc.vector.tensor_copy(h2[1 - s][:, :, C + 1], picks_f[:, 0]).then_inc(tagged.sem, 1)
                        nc.vector.tensor_scalar(tokens[:], tokens[:], float(T), None, ALU.add).then_inc(tagged.sem, 1)
                        nc.vector.tensor_copy(logits[:, bass.ds(c * J, J), :], logit_b).then_inc(kept.sem, 1)
                        nc.vector.tensor_copy(top[:, bass.ds(c * J, J), :], top_b[:, :, 0:2]).then_inc(kept.sem, 1)
                    if has(b):
                        rstd2.wait(dve, b)
                        moments2.wait(dve, b)
                        nc.vector.scalar_tensor_tensor(off2, mv2[:, :, 0], -1.0, r2, ALU.mult,
                                                       ALU.mult).then_inc(off2_ok.sem, 1)
                    if last_routed:
                        dve.wait_ge(zeroed, 2)
                        tagged.wait(dve, B - 1)
                        nc.vector.memset(padding[:, :, C + 1], -1.0).then_inc(padding_ok, 1)
                        nc.vector.tensor_scalar(padding[:, :, C], number[:, 0:(E + SPARE) * SUB], float(P), tokens[:, 0:1],
                                                ALU.mult, ALU.add).then_inc(padding_ok, 1)

                steps(dve, step, behind=2)

                table_link = linker(dve, table_dve)
                base_ok.wait(dve, B - 1)
                nc.vector.tensor_copy(free_i, base[0:1]).then_inc(free_ok, 1)
                table_link(nc.vector.scalar_tensor_tensor(cnt, expert_id[:], -float(REGION), base[:], ALU.mult, ALU.add))
                table_link(nc.vector.tensor_scalar(cnt_i, cnt, float(BLK - 1), None, ALU.add))
                table_link(nc.vector.tensor_scalar(cnt_i, cnt_i, BLK.bit_length() - 1, None, ALU.arith_shift_right))
                table_link(nc.vector.tensor_copy(nblk, cnt_i))
                table_link(nc.vector.memset(no, 0.0))
                table_link(nc.vector.tensor_tensor_scan(cum, nblk, no, 0.0, ALU.add, ALU.add))
                table_link(nc.vector.tensor_scalar(jump, nblk, -float(BLK), float(REGION), ALU.mult, ALU.add))
                table_link(nc.vector.tensor_tensor(reached, number[:].unsqueeze(2).to_broadcast([P, BLOCKS, E]),
                                                   cum.unsqueeze(1).to_broadcast([P, BLOCKS, E]), ALU.is_ge))
                table_link(nc.vector.tensor_tensor(jumps, reached, jump.unsqueeze(1).to_broadcast([P, BLOCKS, E]),
                                                   ALU.mult))
                table_link(nc.vector.tensor_reduce(skipped, jumps, AX.X, ALU.add))
                table_link(nc.vector.scalar_tensor_tensor(row, number[:], float(BLK), skipped, ALU.mult, ALU.add))
                table_link(nc.vector.tensor_reduce(which_f, reached, AX.X, ALU.add))
                table_link(nc.vector.tensor_scalar(which_f, which_f, float(E - 1), None, ALU.min))
                nc.vector.tensor_copy(from_row, row[0:1]).then_inc(table_ok, 1)
                nc.vector.tensor_copy(which, which_f[0:1]).then_inc(table_ok, 1)

            @block.tensor
            def _(pe):
                def product(dst, ways):
                    for i, (wh, wl, k, first) in enumerate(ways):
                        nc.tensor.matmul(dst, wh, hh[:, k, first:first + T], start=i == 0, stop=False)
                        nc.tensor.matmul(dst, wh, hl[:, k, first:first + T], start=False, stop=False)
                        last = nc.tensor.matmul(dst, wl, hh[:, k, first:first + T], start=False,
                                                stop=i == len(ways) - 1)
                    last.then_inc(projected.sem, 1)

                def project(p, m):
                    cols = slice(m * P, (m + 1) * P)
                    product(prj[m][:], [(WPH[:, p, k, cols], WPL[:, p, k, cols], k, HW - T) for k in range(M)])

                def project_f(m):
                    cols = slice(m * P, (m + 1) * P)
                    product(opj[m][:], [(WFH[:, d, k, cols], WFL[:, d, k, cols], k, HW - T - (TAPS - 1) + d)
                                        for d in range(TAPS) for k in range(M)])

                def step(t, s):
                    n, a, b, c = t + 2, t + 1, t, t - 1
                    if has(a):
                        h2_sb.wait(pe, b - 2)
                        for m in range(M):
                            for j in range(J):
                                normed.wait(pe, a, j + 1)
                                last = nc.tensor.transpose(tp[m][:, j * P:(j + 1) * P], xn[:, j, m * P:(m + 1) * P],
                                                           ident[:])
                            last.then_inc(xn_t.sem, 1)
                    if has(b):
                        rms_in.wait(pe, b - 1)
                        sq_ok.wait(pe, b)
                        for j in range(J):
                            for m in range(M):
                                last = nc.tensor.matmul(ssq[:, j:j + 1], sq[:, m, j * P:(j + 1) * P], ones[:, 0:1],
                                                        start=m == 0, stop=m == M - 1)
                        last.then_inc(ssq_ok.sem, 1)
                    if has(b):
                        evac.wait(pe, b, 3 * M)
                        u_lo.wait(pe, b)
                        for j in range(J):
                            dst = opj[j // 2][:, (j % 2) * C:(j % 2 + 1) * C]
                            tok = slice(j * P, (j + 1) * P)
                            for m in range(M):
                                nc.tensor.matmul(dst, uh[:, m, tok], WOH[:, m], start=m == 0, stop=False)
                                nc.tensor.matmul(dst, uh[:, m, tok], WOL[:, m], start=False, stop=False)
                                last = nc.tensor.matmul(dst, ul[:, m, tok], WOH[:, m], start=False, stop=m == M - 1)
                            if j % 2:
                                last.then_inc(o_ok.sem, 1)
                    if has(a):
                        evac.wait(pe, a - 1)
                        h_lo.wait(pe, a)
                        for m in range(M):
                            project(0, m)
                    if has(c):
                        if has(a):
                            h_lo.wait(pe, a)
                        h2_ok.wait(pe, c)
                        for m in range(M):
                            for j in range(J):
                                last = nc.tensor.transpose(tp[m][:, j * P:(j + 1) * P], h2[1 - s][:, j, m * P:(m + 1) * P],
                                                           ident[:])
                            last.then_inc(h2_t.sem, 1)
                    if has(a):
                        attn_ok.wait(pe, b, J // 2)
                        project_f(0)
                    if has(c):
                        h2_sb.wait(pe, c)
                        base_ok.wait(pe, c - 1)
                        rank_ok.wait(pe, c - 1)
                        for j in range(J):
                            for m in range(M):
                                last = nc.tensor.matmul(score[:, j], h2_tsb[:, m, j * P:(j + 1) * P], gate_c[:, m],
                                                        start=m == 0, stop=m == M - 1)
                        last.then_inc(scored.sem, 1)
                    if has(a):
                        attn_ok.wait(pe, b)
                        project_f(1)
                    if has(a):
                        for m in range(M):
                            evac.wait(pe, a, 2 * m + 2)
                            project(1, m)
                    if has(c):
                        hot2_ok.wait(pe, c)
                        score_in.wait(pe, c)
                        for j in range(J):
                            for i in range(j + 1):
                                nc.tensor.matmul(ahead[:, j * E:(j + 1) * E], (before if i == j else ones16)[:],
                                                 hot2[:, i], start=i == 0, stop=i == j)
                        for j in range(J):
                            last = nc.tensor.matmul(total, ones16[:], hot2[:, j], start=j == 0, stop=j == J - 1)
                        last.then_inc(counted.sem, 1)

                steps(pe, step)

        at = [0]
        xin = [place(at, [SUB, ROW]) for _ in range(2)]
        tag = [place(at, [2, SUB]) for _ in range(2)]
        second = [place(at, [SUB]) for _ in range(2)]
        index = [place(at, [SUB], I32) for _ in range(2)]
        xh = [place(at, [M, BLK], F16) for _ in range(2)]
        xl = [place(at, [M, BLK], F16) for _ in range(2)]
        gel = [place(at, [FC, BLK]) for _ in range(2)]
        gh = [place(at, [FC, BLK], F16) for _ in range(2)]
        gl = [place(at, [FC, BLK], F16) for _ in range(2)]
        yo = [place(at, [SUB, C]) for _ in range(2)]
        assert at[0] <= after_padding
        xt_bank, y_bank = bank[0:2], bank[2:4]
        hid = [bank[4:6], bank[6:8]]

        expert_dve = sem("expert_dve")
        spread_ok, exp_ok = sem("spread_ok"), sem("exp_ok")
        rows_in = [count(f"rows_in{s}", 16) for s in range(2)]
        y_out = [count(f"y_out{s}", 16 * SUB) for s in range(2)]
        tag_ok, second_ok, index_ok = count("tag_ok", 1, 2), count("second_ok", 1), count("index_ok", 1)
        rows_t = count("rows_t", 1, 2)
        x_hi, x_lo = count("x_hi", 1, 2), count("x_lo", 1, 2)
        hid_ok = count("hid_ok", 2, 2)
        gelu_ok = count("gelu_ok", 2, 2)
        g_hi, g_lo = count("g_hi", 2, 2), count("g_lo", 2, 2)
        y_ok, y_sb = count("y_ok", 1, 2), count("y_sb", 1, 2)

        def block_steps(eng, step, first=0, end=BLOCKS):
            for i in range(first, 4):
                step(i, i % 2, i // 2)
            pairs = (end - 6) // 2
            with eng.Fori(2, 2 + pairs) as half:
                for s in range(2):
                    step(2 * half + s, s, half)
            for i in range(4 + 2 * pairs, end):
                step(i, i % 2, i // 2)

        def exists(i):
            return not isinstance(i, int) or 0 <= i < BLOCKS

        def reuses(i):
            return not isinstance(i, int) or i >= 2

        with nc.Block() as block:

            @block.gpsimd
            def _(pool):
                def step(i, s, half):
                    pool.wait_ge(index_ok.sem, index_ok.at(i))
                    pool.wait_ge(y_sb.sem, y_sb.at(i))
                    pool.sem_inc(pool_settled, 1)
                    for t in range(SUB):
                        pool.indirect_dma_start(expert_y, bass.IndirectOffsetOnAxis(ap=index[s][:, t:t + 1], axis=0),
                                                yo[s][:, t], None).then_inc(y_out[s].sem, 16)

                block_steps(pool, step)
                for s in range(2):
                    pool.wait_ge(y_out[s].sem, y_out[s].at((BLOCKS - 1 - s) // 2))

            @block.sync
            def _(sp):
                def step(i, s, half):
                    sp.wait_ge(rows_t.sem, rows_t.at(i - 2))
                    sp.wait_ge(tag_ok.sem, tag_ok.at(i - 2))
                    first = sp.value_load(from_row[0:1, bass.ds(i, 1)], min_val=0,
                                          max_val=E * REGION + (SPARE - 1) * BLK)
                    sp.dma_start(xin[s], sorted_x[bass.ds(first, BLK), :].rearrange("(s p) c -> p s c", p=P)
                                 ).then_inc(rows_in[s].sem, 16)

                block_steps(sp, step)

            @block.scalar
            def _(act):
                act.sem_inc(x_hi.sem, 2)
                act.sem_inc(gelu_ok.sem, 4)
                act.sem_inc(y_sb.sem, 2)
                act.wait_ge(spread_ok, 2)
                nc.scalar.activation(flat(spread), flat(spread), ACT.Exp).then_inc(exp_ok, 1)
                nc.scalar.activation(ratio, ratio, ACT.Exp).then_inc(exp_ok, 1)
                nc.scalar.preload_act_table(ACT.Gelu)

                def step(i, s, half):
                    if exists(i + 1):
                        act.wait_ge(rows_t.sem, rows_t.at(i + 1))
                        act.wait_ge(hid_ok.sem, hid_ok.at(i - 1))
                        nc.scalar.activation(flat(xh[1 - s]), xt_bank[1 - s][:], ACT.Copy,
                                             scale=S).then_inc(x_hi.sem, 1)
                    if exists(i):
                        for n in range(2):
                            act.wait_ge(hid_ok.sem, hid_ok.at(i, n + 1))
                            act.wait_ge(g_lo.sem, g_lo.at(i - 2))
                            nc.scalar.activation(flat(gel[s][:, 2 * n:2 * n + 2]), hid[s][n][:], ACT.Gelu,
                                                 scale=1 / S2).then_inc(gelu_ok.sem, 1)
                    if exists(i - 1):
                        act.wait_ge(y_ok.sem, y_ok.at(i - 1))
                        if reuses(i - 1):
                            act.wait_ge(y_out[1 - s].sem, y_out[1 - s].at(half - 2 + s))
                        nc.scalar.activation(flat(yo[1 - s]), y_bank[1 - s][:], ACT.Copy,
                                             scale=1 / S2).then_inc(y_sb.sem, 1)

                block_steps(act, step, -1, BLOCKS + 1)

            @block.vector
            def _(dve):
                dve.sem_inc(x_lo.sem, 2)
                dve.sem_inc(tag_ok.sem, 2)
                dve.sem_inc(g_hi.sem, 4)
                dve.sem_inc(g_lo.sem, 4)
                link = linker(dve, expert_dve)
                nc.vector.tensor_tensor(spread, logits[:], top[:, :, 0:1].to_broadcast([P, TILES, E]),
                                        ALU.subtract).then_inc(spread_ok, 1)
                nc.vector.tensor_tensor(ratio, top[:, :, 1], top[:, :, 0], ALU.subtract).then_inc(spread_ok, 1)

                def step(i, s, half):
                    if exists(i + 1):
                        dve.wait_ge(x_hi.sem, x_hi.at(i + 1))
                        dve.wait_ge(hid_ok.sem, hid_ok.at(i - 1))
                        nc.vector.scalar_tensor_tensor(flat(xl[1 - s]), xt_bank[1 - s][:], S, flat(xh[1 - s]), ALU.mult,
                                                       ALU.subtract).then_inc(x_lo.sem, 1)
                        dve.wait_ge(rows_in[1 - s].sem, rows_in[1 - s].at(half + s))
                        if reuses(i + 1):
                            dve.wait_ge(index_ok.sem, index_ok.at(i - 1))
                        nc.vector.tensor_copy(tag[1 - s].rearrange("p w t -> p t w"), xin[1 - s][:, :, C:ROW]
                                              ).then_inc(tag_ok.sem, 1)
                    if exists(i):
                        dve.wait_ge(tag_ok.sem, tag_ok.at(i))
                        nc.vector.tensor_scalar(second[s], tag[s][:, 1], which_f[:, bass.ds(i, 1)], float(N),
                                                ALU.not_equal, ALU.mult).then_inc(second_ok.sem, 1)
                        for n in range(2):
                            dve.wait_ge(gelu_ok.sem, gelu_ok.at(i, n + 1))
                            dve.wait_ge(y_ok.sem, y_ok.at(i - 2))
                            nc.vector.tensor_scalar(flat(gh[s][:, 2 * n:2 * n + 2]), flat(gel[s][:, 2 * n:2 * n + 2]),
                                                    S, None, ALU.mult).then_inc(g_hi.sem, 1)
                        for n in range(2):
                            dve.wait_ge(g_hi.sem, g_hi.at(i, n + 1))
                            nc.vector.scalar_tensor_tensor(
                                flat(gl[s][:, 2 * n:2 * n + 2]), flat(gel[s][:, 2 * n:2 * n + 2]), S,
                                flat(gh[s][:, 2 * n:2 * n + 2]), ALU.mult, ALU.subtract).then_inc(g_lo.sem, 1)
                        dve.wait_ge(second_ok.sem, second_ok.at(i))
                        if reuses(i):
                            dve.wait_ge(y_out[s].sem, y_out[s].at(half - 1))
                        nc.vector.tensor_tensor(index[s], second[s], tag[s][:, 0], ALU.add).then_inc(index_ok.sem, 1)

                block_steps(dve, step, -1)
                dve.wait_ge(exp_ok, 2)
                link(nc.vector.tensor_reduce(denom, spread, AX.X, ALU.add))
                link(nc.vector.reciprocal(prob[:, 0], denom))
                link(nc.vector.tensor_tensor(prob[:, 1], prob[:, 0], ratio, ALU.mult))

            @block.tensor
            def _(pe):
                pe.sem_inc(rows_t.sem, 2)
                pe.sem_inc(hid_ok.sem, 4)
                pe.sem_inc(y_ok.sem, 2)

                def step(i, s, half):
                    if exists(i + 1):
                        pe.wait_ge(rows_in[1 - s].sem, rows_in[1 - s].at(half + s))
                        pe.wait_ge(x_lo.sem, x_lo.at(i - 1))
                        for m in range(M):
                            for t in range(SUB):
                                last = nc.tensor.transpose(xt_bank[1 - s][:, m * BLK + t * P:m * BLK + (t + 1) * P],
                                                           xin[1 - s][:, t, m * P:(m + 1) * P], ident[:])
                        last.then_inc(rows_t.sem, 1)
                    if exists(i):
                        e = pe.value_load(which[0:1, bass.ds(i, 1)], min_val=0, max_val=E - 1)
                        pe.wait_ge(x_lo.sem, x_lo.at(i))
                        for n in range(2):
                            pe.wait_ge(gelu_ok.sem, gelu_ok.at(i - 2, n + 1))
                            for f in (2 * n, 2 * n + 1):
                                dst = hid[s][n][:, (f - 2 * n) * BLK:(f - 2 * n + 1) * BLK]
                                for m in range(M):
                                    cols = bass.ds(e * F + (m * E * F + f * P), P)
                                    nc.tensor.matmul(dst, WEH[:, cols], xh[s][:, m], start=m == 0, stop=False)
                                    nc.tensor.matmul(dst, WEH[:, cols], xl[s][:, m], start=False, stop=False)
                                    last = nc.tensor.matmul(dst, WEL[:, cols], xh[s][:, m], start=False,
                                                            stop=m == M - 1)
                            last.then_inc(hid_ok.sem, 1)
                    if exists(i - 1):
                        r = 1 - s
                        e = pe.value_load(which[0:1, bass.ds(i - 1, 1)], min_val=0, max_val=E - 1)
                        pe.wait_ge(g_lo.sem, g_lo.at(i - 1))
                        pe.wait_ge(y_sb.sem, y_sb.at(i - 3))
                        for t in range(SUB):
                            dst = y_bank[r][:, t * C:(t + 1) * C]
                            tok = slice(t * P, (t + 1) * P)
                            for f in range(FC):
                                cols = bass.ds(e * C + (W2_AT + f * E * C), C)
                                nc.tensor.matmul(dst, gh[r][:, f, tok], WEH[:, cols], start=f == 0, stop=False)
                                nc.tensor.matmul(dst, gh[r][:, f, tok], WEL[:, cols], start=False, stop=False)
                                last = nc.tensor.matmul(dst, gl[r][:, f, tok], WEH[:, cols], start=False,
                                                        stop=f == FC - 1)
                        last.then_inc(y_ok.sem, 1)

                block_steps(pe, step, -1, BLOCKS + 1)

        DEPTH = 4
        at = [0]
        got = [place(at, [2 * J, C]) for _ in range(DEPTH)]
        gain = [place(at, [C]) for _ in range(DEPTH)]
        got_in = [count(f"got_in{s}", 48) for s in range(DEPTH)]
        stored = sem("stored")
        first_ok, both_ok = count("first_ok", J), count("both_ok", J)
        gained, summed = count("gained", 1), count("summed", 1, DEPTH)

        with nc.Block() as block:

            @block.scalar
            def _(act):
                with act.Fori(0, B // DEPTH) as q:
                    for s in range(DEPTH):
                        b = DEPTH * q + s
                        act.wait_ge(got_in[s].sem, got_in[s].at(q))
                        for j in range(J):
                            nc.scalar.activation(got[s][:, j], got[s][:, j], ACT.Copy,
                                                 scale=prob[:, 0, bass.ds(b * J + j, 1)]).then_inc(first_ok.sem, 1)

            @block.vector
            def _(dve):
                with dve.Fori(0, B // DEPTH) as q:
                    for s in range(DEPTH):
                        b = DEPTH * q + s
                        dve.wait_ge(got_in[s].sem, got_in[s].at(q))
                        for j in range(J):
                            dve.wait_ge(first_ok.sem, first_ok.at(b, j + 1))
                            nc.vector.scalar_tensor_tensor(got[s][:, j], got[s][:, J + j],
                                                           prob[:, 1, bass.ds(b * J + j, 1)], got[s][:, j], ALU.mult,
                                                           ALU.add).then_inc(both_ok.sem, 1)
                        dve.wait_ge(both_ok.sem, both_ok.at(b))
                        nc.vector.tensor_tensor(got[s][:, 0:J], got[s][:, 0:J],
                                                gain[s].unsqueeze(1).to_broadcast([P, J, C]),
                                                ALU.mult).then_inc(gained.sem, 1)

            @block.gpsimd
            def _(pool):
                pool.sem_inc(summed.sem, DEPTH)
                with pool.Fori(0, B // DEPTH) as q:
                    for s in range(DEPTH):
                        b = DEPTH * q + s
                        pool.wait_ge(gained.sem, gained.at(b))
                        pool.sem_inc(pool_settled, 1)
                        xb = X[:, bass.ds(b * J, J), :]
                        nc.gpsimd.tensor_tensor(xb, xb, got[s][:, 0:J], ALU.add).then_inc(summed.sem, 1)

            @block.sync
            def _(sp):
                def load(b, s):
                    sp.wait_ge(summed.sem, summed.at(b - DEPTH))
                    for i in range(2):
                        sp.dma_start(got[s][:, i * J:(i + 1) * J],
                                     expert_y[bass.ds(b * T + i * N, T), :].rearrange("(j p) c -> p j c", p=P)
                                     ).then_inc(got_in[s].sem, 16)
                    sp.dma_start(gain[s], mod_rows[bass.ds(b, 1), 3 * C:4 * C].to_broadcast([P, C])
                                 ).then_inc(got_in[s].sem, 16)

                def store(b):
                    sp.wait_ge(summed.sem, summed.at(b))
                    sp.dma_start(out[bass.ds(b * T, T), :].rearrange("(j p) c -> p j c", p=P),
                                 X[:, bass.ds(b * J, J), :]).then_inc(stored, 16)

                for s in range(DEPTH):
                    load(s, s)
                with sp.Fori(0, B // DEPTH - 1) as q:
                    for s in range(DEPTH):
                        store(DEPTH * q + s)
                        load(DEPTH * (q + 1) + s, s)
                for b in range(B - DEPTH, B):
                    store(b)
                sp.wait_ge(stored, 16 * B)


_IN = {
    "x": "L0_attn_x", "wi": "L0_attn_Wi", "wf": "L0_attn_Wf", "wg": "L0_attn_Wg", "conv_i": "L0_attn_conv_i",
    "conv_f": "L0_attn_conv_f", "gnorm": "L0_attn_g_norm_weight", "wo": "L0_attn_Wo", "gamma": "L0_ffn_ln_gamma",
    "beta": "L0_ffn_ln_beta", "gate": "L0_ffn_gate_w", "w1": "L0_ffn_w1", "w2": "L0_ffn_w2", "c_t": "L0_c",
    "wmod": "L0_wmod",
}


def lay_out(inputs):
    a = {k: np.asarray(inputs[v]) for k, v in _IN.items()}
    a["x"] = a["x"].reshape(N, C)
    for name in ("gnorm", "gamma", "beta"):
        a[name] = a[name].reshape(M, P).T
    a["gate"] = a["gate"].T
    a["c_t"] = a["c_t"].T
    a["conv_f_rows"] = a["conv_f"].T.reshape(1, TAPS * C)
    w1 = a.pop("w1").transpose(2, 0, 1).reshape(M, P, E * F // STAGE, STAGE).transpose(0, 2, 1, 3)
    w2 = a.pop("w2").transpose(2, 0, 1).reshape(FC, P, E * C // STAGE, STAGE).transpose(0, 2, 1, 3)
    a["w12"] = np.concatenate([w1.reshape(-1, STAGE), w2.reshape(-1, STAGE)])
    return {k: np.ascontiguousarray(v) for k, v in a.items()}


def kernel(**inputs):
    import concourse.bacc as bacc
    from concourse.bass_utils import run_bass_kernel_spmd

    nc = bacc.Bacc("TRN2", target_bir_lowering=False, num_devices=1)
    arrays = lay_out(inputs)
    aps = {k: nc.dram_tensor(f"in_{k}", a.shape, mybir.dt.from_np(a.dtype), kind="ExternalInput").ap()
           for k, a in arrays.items()}
    out = nc.dram_tensor("out_x", (N, C), F32, kind="ExternalOutput").ap()
    build(nc, out=out, **aps)
    got = run_bass_kernel_spmd(nc, [{f"in_{k}": a for k, a in arrays.items()}], core_ids=[0])
    return got.results[0]["out_x"].reshape(B, T, C)
```
